# Optimizing a Trainium2 kernel written in Bass

```python
import numpy as np
import jax
import jax.numpy as jnp

def _softmax(x, axis=-1):
    return jax.nn.softmax(x, axis=axis)
def _gelu(x):
    return jax.nn.gelu(x, approximate=True)
def _silu(x):
    return jax.nn.silu(x)
def _sigmoid(x):
    return jax.nn.sigmoid(x)
def _layernorm(x, axis=-1, eps=1e-5):
    m = jnp.mean(x, axis=axis, keepdims=True)
    v = jnp.var(x, axis=axis, keepdims=True)
    return (x - m) / jnp.sqrt(v + eps)
def _scatter_add(tgt, idx, src, axis=0):
    return tgt.at[idx].add(src)
def _segment_sum(src, seg, n):
    return jax.ops.segment_sum(src, seg, n)

kernel_name = 'mk_conv_preact_d1_conv_nchw512_98533f'

def setup_inputs(seed: int = 0):
    np.random.seed(seed)
    _w = jnp.asarray
    def _rec_inputs():
        import jax
        import jax.numpy as jnp
        _gk = jax.random.key(seed)
        x = -0.000125 + 0.9999 * jax.random.normal(jax.random.fold_in(_gk, 1), (16, 512, 64, 64), jnp.float32)
        return x
    x = _rec_inputs()
    def _L0_conv_setup():
        import jax, jax.numpy as jnp
        import numpy as np
        B, C, H, W = (16, 512, 64, 64)
        D = C // 8
        key = jax.random.key(seed)
        ks = jax.random.split(key, 8)
        s = 0.02
        x = jax.random.normal(ks[0], (B, C, H, W), dtype=jnp.float32)
        Wq = jax.random.normal(ks[1], (D, C), dtype=jnp.float32) * s
        bq = jnp.zeros((D,), dtype=jnp.float32)
        Wk = jax.random.normal(ks[2], (D, C), dtype=jnp.float32) * s
        bk = jnp.zeros((D,), dtype=jnp.float32)
        Wv = jax.random.normal(ks[3], (C, C), dtype=jnp.float32) * s
        bv = jnp.zeros((C,), dtype=jnp.float32)
        gamma = jnp.full((1,), 0.5, dtype=jnp.float32)
        return {'x': x, 'Wq': Wq, 'bq': bq, 'Wk': Wk, 'bk': bk, 'Wv': Wv, 'bv': bv, 'gamma': gamma}
    _L0_conv_all = _L0_conv_setup()
    _L0_conv_in = {k: v for k, v in _L0_conv_all.items() if k in ('Wq', 'bq', 'Wk', 'bk', 'Wv', 'bv', 'gamma', )}
    del _L0_conv_all

    return {
        "x": x,
        "L0_conv_Wq": _L0_conv_in["Wq"],
        "L0_conv_bq": _L0_conv_in["bq"],
        "L0_conv_Wk": _L0_conv_in["Wk"],
        "L0_conv_bk": _L0_conv_in["bk"],
        "L0_conv_Wv": _L0_conv_in["Wv"],
        "L0_conv_bv": _L0_conv_in["bv"],
        "L0_conv_gamma": _L0_conv_in["gamma"],
    }

def reference(x, L0_conv_Wq, L0_conv_bq, L0_conv_Wk, L0_conv_bk, L0_conv_Wv, L0_conv_bv, L0_conv_gamma):
    import jax
    import jax.numpy as jnp
    def _L0_conv_ref(x, Wq, bq, Wk, bk, Wv, bv, gamma):
        import jax, jax.numpy as jnp
        import numpy as np
        B, C, H, W = (16, 512, 64, 64)
        D = C // 8
        b, c, h, w = x.shape
        n = h * w
        xf = x.reshape(b, c, n)
        q = jnp.einsum('bcn,dc->bdn', xf, Wq) + bq[None, :, None]
        k = jnp.einsum('bcn,dc->bdn', xf, Wk) + bk[None, :, None]
        v = jnp.einsum('bcn,oc->bon', xf, Wv) + bv[None, :, None]
        vk = jnp.einsum('bcn,bdn->bcd', v, k)
        out = jnp.einsum('bcd,bdn->bcn', vk, q)
        out = out.reshape(b, c, h, w)
        return gamma * out + x

    def _gn(v, G=32, eps=1e-5):
        B_, C_, H_, W_ = v.shape
        g = v.reshape(B_, G, C_ // G, H_, W_)
        m = jnp.mean(g, axis=(2, 3, 4), keepdims=True)
        s = jnp.var(g, axis=(2, 3, 4), keepdims=True)
        return ((g - m) / jnp.sqrt(s + eps)).reshape(v.shape)

    def _ln_c(v, eps=1e-6):
        m = jnp.mean(v, axis=1, keepdims=True)
        s = jnp.var(v, axis=1, keepdims=True)
        return (v - m) / jnp.sqrt(s + eps)

    def _ln_t(v, eps=1e-5):
        m = jnp.mean(v, axis=-1, keepdims=True)
        s = jnp.var(v, axis=-1, keepdims=True)
        return (v - m) / jnp.sqrt(s + eps)

    def _to_tokens(v):
        B_, C_, H_, W_ = v.shape
        return v.reshape(B_, C_, H_ * W_).transpose(0, 2, 1)
    def _from_tokens(t, like):
        B_, C_, H_, W_ = like.shape
        return t.transpose(0, 2, 1).reshape(B_, C_, H_, W_)

    x = x + _L0_conv_ref(_gn(x), L0_conv_Wq, L0_conv_bq, L0_conv_Wk, L0_conv_bk, L0_conv_Wv, L0_conv_bv, L0_conv_gamma)
    return x


_drawn_inputs = setup_inputs


def setup_inputs(seed=0):
    import zlib

    import numpy as np

    out = dict(_drawn_inputs(seed))
    spreads = {'L0_conv_bq': (0.0, 0.1), 'L0_conv_bk': (0.0, 0.1), 'L0_conv_bv': (0.0, 0.1)}
    factors = {}
    for name, (base, spread) in spreads.items():
        noise = np.random.default_rng([zlib.crc32(name.encode()), seed]).standard_normal(out[name].shape)
        drawn = base * np.exp(spread * noise) if base else spread * noise
        out[name] = jnp.asarray(drawn.astype(out[name].dtype))
    for name, factor in factors.items():
        out[name] = (out[name] * factor).astype(out[name].dtype)
    return out
```

```python
import concourse.bass as bass
from concourse import mybir
from contextlib import ExitStack


def bass_groupnorm_linear_attention(
    nc: bass.Bass,
    x: bass.AP,
    Wq: bass.AP,
    bq: bass.AP,
    Wk: bass.AP,
    bk: bass.AP,
    Wv: bass.AP,
    bv: bass.AP,
    gamma: bass.AP,
    out: bass.AP,
):
    f32, f32r = mybir.dt.float32, mybir.dt.float32r
    ALU = mybir.AluOpType
    ACT = mybir.ActivationFunctionType

    P = 128
    IMAGES, C, HEIGHT, WIDTH = x.shape
    N = HEIGHT * WIDTH
    D = Wq.shape[0]
    CC = C // P
    TN = 512
    TILES = N // TN
    CHUNKS = TN // P
    STEPS = TILES * CHUNKS
    GROUP = C // 32
    EPS = 1e-5
    LAG = CHUNKS
    assert 2 * D == P and CC == CHUNKS and IMAGES % 2 == 0

    STEP_SUM = LAG
    STEP_J = LAG + 1
    STEP_VK = LAG + 2
    STEP_OUT = LAG + 3
    UNITS = TILES * CC
    UNITS_AT = [0] * STEPS
    left = UNITS
    for s in range(STEP_OUT, STEPS):
        UNITS_AT[s] = min(2, left)
        left -= UNITS_AT[s]
    UNITS_BEFORE = [sum(UNITS_AT[:s]) for s in range(STEPS + 1)]
    STATS_AT = {min(STEPS - 1, STEP_OUT + 7 + (5 * t) // 2): [] for t in range(TILES)}
    for t in range(TILES):
        STATS_AT[min(STEPS - 1, STEP_OUT + 7 + (5 * t) // 2)].append(t)

    RING_STATS, RING_SMALL, RING_OUT = 4, 2, UNITS
    RING = RING_STATS + RING_SMALL + RING_OUT

    x_v = x.rearrange("b (c p) h w -> b p c (h w)", p=P)
    out_v = out.rearrange("b (c p) h w -> b p c (h w)", p=P)

    ctx = ExitStack()
    with ctx:
        def sb(name, shape, dt=f32):
            return ctx.enter_context(nc.sbuf_tensor(name, shape, dt))

        def pb(name, shape, dt=f32):
            return ctx.enter_context(nc.psum_tensor(name, shape, dt))

        def sem(name):
            return ctx.enter_context(nc.semaphore(name))

        X = [sb(f"X{i}", [P, CC, N]) for i in range(2)]
        q_hl = [sb(f"q_hl{i}", [P, N], f32r) for i in range(2)]
        xT_hi = sb("xT_hi", [P, CHUNKS, C], f32r)
        xT_lo = sb("xT_lo", [P, CHUNKS, C], f32r)
        kT_hl = [sb(f"kT_hl{i}", [P, CHUNKS, P], f32r) for i in range(2)]
        k_row = sb("k_row", [P, TN])
        k_nat = k_row[D:P, :]
        bv_row = k_row[0:1, 0:C]
        W_raw = sb("W_raw", [P, CC, P])
        W_fold = [sb(f"W_fold{i}", [P, CC, P]) for i in range(2)]
        WvT = sb("WvT", [P, CC, C])
        ST = sb("ST", [P, C])
        SC = ST[:, :].rearrange("p (c j) -> p c j", j=P)
        VK_hi = sb("VK_hi", [P, C], f32r)
        VK_lo = sb("VK_lo", [P, C], f32r)
        identity = sb("identity", [P, P])
        fold_halves = sb("fold_halves", [P, P])
        group_mean = sb("group_mean", [P, P])
        ones = sb("ones", [P, P])
        bn = sb("bn", [P, CC, TILES, 6])
        mv = sb("mv", [P, CC, 2])
        dev = sb("dev", [P, CC])
        e2 = sb("e2", [P, CC])
        gvar = sb("gvar", [P, CC])
        root = sb("root", [P, CC])
        r0 = sb("r0", [P, CC])
        r1 = sb("r1", [P, CC])
        beta_mean = sb("beta_mean", [P, CC, 2])
        b_raw = sb("b_raw", [P, 1])
        gamma_col = sb("gamma_col", [P, 1])
        kmean = sb("kmean", [P, 1])
        ksum_rows = sb("ksum_rows", [P, P])
        neg_mean = [sb(f"neg_mean{i}", [P, CC]) for i in range(2)]
        scale_a = [sb(f"scale_a{i}", [P, CC]) for i in range(2)]
        scale_a1 = [sb(f"scale_a1{i}", [P, CC]) for i in range(2)]
        beta = [sb(f"beta{i}", [P, CC]) for i in range(2)]
        b_fold = [sb(f"b_fold{i}", [P, 1]) for i in range(2)]
        ksum_all = [sb(f"ksum_all{i}", [P, P]) for i in range(2)]

        Wv_nat = X[1][:, 0, 0:CC * C].rearrange("p (o c) -> p o c", c=C)
        W_nat = X[1][:, 1, 0:C]

        ps_qk = [pb(f"ps_qk{i}", [P, TN]) for i in range(2)]
        ps_xT = [pb(f"ps_xT{i}", [P, C]) for i in range(2)]
        ps_kT = pb("ps_kT", [P, TN])
        ps_S = pb("ps_S", [P, C])
        ps_ring = [pb(f"ps_ring{i}", [P, TN]) for i in range(2)]

        s_weights = sem("s_weights")
        s_x = [[sem(f"s_x{i}_{t}") for t in range(TILES)] for i in range(2)]
        s_y = [sem(f"s_y{t}") for t in range(TILES)]
        s_const0 = sem("s_const0")
        s_const = sem("s_const")
        s_wt = sem("s_wt")
        s_wc = sem("s_wc")
        s_bn = sem("s_bn")
        s_stat = sem("s_stat")
        s_root = sem("s_root")
        s_fold = sem("s_fold")
        s_proj = sem("s_proj")
        s_xT = sem("s_xT")
        s_kT = sem("s_kT")
        s_S = sem("s_S")
        s_k = sem("s_k")
        s_qhi = sem("s_qhi")
        s_qlo = sem("s_qlo")
        s_kThi = sem("s_kThi")
        s_kTlo = sem("s_kTlo")
        s_xThi = sem("s_xThi")
        s_xTlo = sem("s_xTlo")
        s_sum = sem("s_sum")
        s_ring = sem("s_ring")
        s_free = sem("s_free")
        s_res = sem("s_res")

        s_passed = sem("s_passed")

        block = ctx.enter_context(nc.Block())

        def tile_no(p, t):
            return p * TILES + t

        def step_no(p, s):
            return p * STEPS + s

        def settle(eng):
            eng.sem_inc(s_passed, 1)

        def is_int(v):
            return isinstance(v, int)

        def ring_stats(p, k):
            if is_int(p) and p == 0:
                return k
            return p * RING + (RING_STATS - RING) + k

        def ring_small(p, k):
            return ring_stats(p, (0 if is_int(p) and p == IMAGES else RING_STATS) + k)

        def ring_out(p, u):
            return ring_small(p, RING_SMALL + u)

        STAT = 11
        SMALL = 3

        def periods(eng, period):
            period(0, 0)
            with eng.Fori(0, IMAGES // 2 - 1) as it:
                period(it * 2 + 1, 1)
                period(it * 2 + 2, 0)
            period(IMAGES - 1, 1)
            period(IMAGES, 0)

        def wait_count(eng, s, value):
            if not is_int(value) or value > 0:
                eng.wait_ge(s, value)

        @block.sync
        def _(sp):
            sp.dma_start(W_nat[0:D, :], Wq).then_inc(s_weights, 16)
            sp.dma_start(W_nat[D:P, :], Wk).then_inc(s_weights, 16)
            sp.dma_start(Wv_nat, Wv.rearrange("(o p) c -> p o c", p=P)).then_inc(s_weights, 16)
            with nc.allow_non_contiguous_dma(reason="one bias per partition"):
                sp.dma_start(b_raw[0:D, :], bq.rearrange("(p a) -> p a", a=1)).then_inc(s_weights, 16)
                sp.dma_start(b_raw[D:P, :], bk.rearrange("(p a) -> p a", a=1)).then_inc(s_weights, 16)
                sp.dma_start(gamma_col[:, :], gamma.rearrange("(a n) -> a n", a=1).to_broadcast([P, 1]))\
                    .then_inc(s_weights, 16)
            sp.dma_start(bv_row, bv.rearrange("(a n) -> a n", a=1)).then_inc(s_weights, 16)

            def tile(buffer, t):
                return X[buffer][:, :, t * TN:(t + 1) * TN]

            def load(p, buffer, t):
                sp.dma_start(tile(buffer, t), x_v[p, :, :, t * TN:(t + 1) * TN])\
                    .then_inc(s_x[buffer][t], 16)

            for t in range(TILES):
                load(0, 0, t)
            sp.wait_ge(s_wc, CC + 1)
            for t in range(TILES):
                load(1, 1, t)

            def period(p, parity):
                if is_int(p) and p == 0:
                    return
                other = 1 - parity
                loads = not (is_int(p) and p >= IMAGES - 1)
                for t in range(TILES):
                    sp.wait_ge(s_free, ring_out(p, (t + 1) * CC))
                    sp.dma_start(out_v[p - 1, :, :, t * TN:(t + 1) * TN], tile(other, t)).then_inc(s_y[t], 16)
                    if loads and t >= 1:
                        sp.wait_ge(s_y[t - 1], p * 16)
                        load(p + 1, other, t - 1)
                if loads:
                    sp.wait_ge(s_y[TILES - 1], p * 16)
                    load(p + 1, other, TILES - 1)

            periods(sp, period)
            for t in range(TILES):
                sp.wait_ge(s_y[t], IMAGES * 16)

        @block.gpsimd
        def _(pool):
            nc.gpsimd.memset(identity[:, :], 0.0).then_inc(s_const0, 1)
            nc.gpsimd.memset(group_mean[:, :], 1.0 / GROUP).then_inc(s_const0, 1)
            nc.gpsimd.memset(ones[:, :], 1.0).then_inc(s_const0, 1)
            pool.wait_ge(s_const0, 3)
            nc.gpsimd.affine_select(out=identity[:, :], in_=identity[:, :], compare_op=ALU.not_equal, fill=1.0,
                                    base=0, pattern=[[-1, P]], channel_multiplier=1).then_inc(s_const, 1)
            gm = group_mean[:, :].rearrange("p (g c) -> p g c", c=GROUP)
            nc.gpsimd.affine_select(out=gm, in_=gm, compare_op=ALU.is_ge, fill=0.0, base=0,
                                    pattern=[[-GROUP, P // GROUP], [0, GROUP]], channel_multiplier=1)\
                .then_inc(s_const0, 1)
            pool.wait_ge(s_const0, 4)
            nc.gpsimd.affine_select(out=gm, in_=gm, compare_op=ALU.is_ge, fill=0.0, base=GROUP - 1,
                                    pattern=[[GROUP, P // GROUP], [0, GROUP]], channel_multiplier=-1)\
                .then_inc(s_const, 1)

            def period(p, parity):
                if is_int(p) and p == IMAGES:
                    return
                if is_int(p) and p == 0:
                    pool.wait_ge(s_wc, 1)
                pool.wait_ge(s_stat, p * STAT + 9)
                settle(pool)
                for c in range(CC):
                    nc.gpsimd.tensor_scalar(W_fold[parity][:, c, :], W_raw[:, c, :], scale_a[parity][:, c:c + 1],
                                            1.0, ALU.mult, ALU.mult).then_inc(s_fold, 1)
                pool.wait_ge(s_stat, p * STAT + 10)
                for t in range(TILES):
                    pool.wait_ge(s_proj, tile_no(p, t) + 1)
                    pool.wait_ge(s_xT, step_no(p, (t + 1) * CHUNKS))
                    settle(pool)
                    for c in range(CC):
                        xs = X[parity][:, c, t * TN:(t + 1) * TN]
                        nc.gpsimd.tensor_scalar(xs, xs, scale_a1[parity][:, c:c + 1], beta[parity][:, c:c + 1],
                                                ALU.mult, ALU.add).then_inc(s_res, 1)

            periods(pool, period)

        @block.scalar
        def _(act):
            def tile_out(p, parity, t):
                n = tile_no(p, t)
                bank = ps_qk[t % 2]
                if t == 0:
                    act.wait_ge(s_stat, p * STAT + 11)
                act.wait_ge(s_proj, n + 1)
                wait_count(act, s_kT, n)
                nc.scalar.activation(k_nat, bank[D:P, :], ACT.Identity, bias=b_fold[parity][D:P, :]).then_inc(s_k, 1)
                nc.scalar.activation(q_hl[parity][0:D, t * TN:(t + 1) * TN], bank[0:D, :], ACT.Identity,
                                     bias=b_fold[parity][0:D, :]).then_inc(s_qhi, 1)

            def kT_high(p, t):
                n = tile_no(p, t)
                act.wait_ge(s_kT, n + 1)
                wait_count(act, s_S, (n - 1) * CHUNKS)
                nc.scalar.activation(kT_hl[t % 2][:, :, 0:D], ps_kT[:, 0:CHUNKS * D].rearrange("p (j d) -> p j d", d=D),
                                     ACT.Copy).then_inc(s_kThi, 1)

            def xT_high(p, s):
                g = step_no(p, s)
                act.wait_ge(s_xT, g + 1)
                wait_count(act, s_S, g - LAG + 1)
                nc.scalar.activation(xT_hi[:, s % CHUNKS, :], ps_xT[s % 2][:, :], ACT.Copy).then_inc(s_xThi, 1)

            def period(p, parity):
                tail = is_int(p) and p == IMAGES
                first = is_int(p) and p == 0
                for s in range(LAG if tail else STEPS):
                    t, j = s // CHUNKS, s % CHUNKS
                    if j == 0 and not (first and s == 0):
                        tp, tt, par = (p, t - 1, parity) if t else (p - 1, TILES - 1, 1 - parity)
                        tile_out(tp, par, tt)
                        kT_high(tp, tt)
                    if s == 0 and not tail:
                        act.wait_ge(s_free, ring_stats(p, 1) + 1)
                        nc.scalar.activation(root[:, :], gvar[:, :], ACT.Sqrt).then_inc(s_root, 1)
                    if not tail:
                        xT_high(p, s)

            periods(act, period)

        @block.tensor
        def _(pe):
            def ring(number, k, parts):
                wait_count(pe, s_free, number - 1)
                bank = ps_ring[k % 2]
                for columns, lhsT, rhs, start, stop in parts:
                    last = nc.tensor.matmul(bank[:, columns], lhsT, rhs, start=start, stop=stop)
                last.then_inc(s_ring, 1)

            pe.wait_ge(s_const, 2)
            pe.wait_ge(s_weights, 16 * 7)
            for c in range(CC):
                last = nc.tensor.transpose(ps_xT[0][:, c * P:(c + 1) * P], W_nat[:, c * P:(c + 1) * P],
                                           identity[:, :])
            last.then_inc(s_wt, 1)
            for c in range(CC):
                wait_count(pe, s_wc, c)
                for o in range(CC):
                    last = nc.tensor.transpose(ps_xT[(c + 1) % 2][:, o * P:(o + 1) * P],
                                               Wv_nat[:, o, c * P:(c + 1) * P], identity[:, :])
                last.then_inc(s_wt, 1)
            pe.wait_ge(s_wc, CC + 1)

            def project(p, parity, t, c):
                if c == 0:
                    n = tile_no(p, t)
                    wait_count(pe, s_k, n - 1)
                    wait_count(pe, s_qlo, n - 1)
                if t == 0:
                    pe.wait_ge(s_fold, p * CC + c + 1)
                mm = nc.tensor.matmul(ps_qk[t % 2][:, :], W_fold[parity][:, c, :],
                                      X[parity][:, c, t * TN:(t + 1) * TN], start=(c == 0), stop=(c == CC - 1))
                if c == CC - 1:
                    mm.then_inc(s_proj, 1)

            def transpose_x(p, parity, s):
                g = step_no(p, s)
                wait_count(pe, s_xTlo, g - 1)
                for c in range(CC):
                    last = nc.tensor.transpose(ps_xT[s % 2][:, c * P:(c + 1) * P],
                                               X[parity][:, c, s * P:(s + 1) * P], identity[:, :])
                last.then_inc(s_xT, 1)

            def transpose_k(p, t):
                n = tile_no(p, t)
                pe.wait_ge(s_k, n + 1)
                wait_count(pe, s_kTlo, n)
                settle(pe)
                for j in range(CHUNKS):
                    last = nc.tensor.transpose(ps_kT[:, j * D:(j + 1) * D], k_nat[:, j * P:(j + 1) * P],
                                               identity[D:P, D:P])
                last.then_inc(s_kT, 1)

            def x_kT(p, s):
                t, j = s // CHUNKS, s % CHUNKS
                if j == 0:
                    pe.wait_ge(s_kTlo, tile_no(p, t) + 1)
                if s == 0:
                    wait_count(pe, s_sum, (p - 1) * SMALL + 1)
                pe.wait_ge(s_xTlo, step_no(p, s) + 1)
                nc.tensor.matmul(ps_S[:, :], kT_hl[t % 2][:, j, :], xT_hi[:, j, :], start=(s == 0), stop=False)
                nc.tensor.matmul(ps_S[:, :], kT_hl[t % 2][:, j, :], xT_lo[:, j, :], start=False,
                                 stop=(s == STEPS - 1)).then_inc(s_S, 1)

            def output_unit(p, other, u):
                t, c = u // CC, u % CC
                if u == 0:
                    pe.wait_ge(s_free, ring_out(p, 0))
                    pe.wait_ge(s_qlo, p * TILES)
                q = q_hl[other][:, t * TN:(t + 1) * TN]
                everything = slice(0, TN)
                ring(ring_out(p, u), u, [(everything, VK_hi[:, c * P:(c + 1) * P], q, True, False),
                                      (everything, VK_lo[:, c * P:(c + 1) * P], q, False, True)])

            def period(p, parity):
                tail = is_int(p) and p == IMAGES
                first = is_int(p) and p == 0
                other = 1 - parity
                for s in range(STEPS):
                    t, j = s // CHUNKS, s % CHUNKS
                    if not tail:
                        if s == 0:
                            pe.wait_ge(s_stat, p * STAT + 1)
                            ring(ring_stats(p, 0), 0, [(slice(0, CC), group_mean[:, :], mv[:, :, 0], True, True)])
                        if s == 2:
                            project(p, parity, 0, 0)
                            project(p, parity, 0, 1)
                        if s >= 2:
                            project(p, parity, t, j)
                    if j == 0 and not (first and s == 0) and s < (LAG if tail else STEPS):
                        transpose_k(*((p, t - 1) if t else (p - 1, TILES - 1)))
                    if not tail:
                        transpose_x(p, parity, s)
                        if s == 0:
                            pe.wait_ge(s_stat, p * STAT + 4)
                            ring(ring_stats(p, 1), 1, [(slice(0, CC), group_mean[:, :], e2[:, :], True, True)])
                    if s == STEP_J and not first:
                        pe.wait_ge(s_sum, (p - 1) * SMALL + 1)
                        ring(ring_small(p, 0), 0, [(slice(c * P, (c + 1) * P), ST[:, c * P:(c + 1) * P],
                                                 fold_halves[:, :], True, True) for c in range(CC)])
                    if s == STEP_VK and not first:
                        pe.wait_ge(s_sum, (p - 1) * SMALL + 2)
                        ring(ring_small(p, 1), 1,
                             [(slice(0, C), SC[:, c, :], WvT[:, c, :], c == 0, False) for c in range(CC)]
                             + [(slice(0, C), ksum_all[other][0:1, :], bv_row, False, True)])
                    if not first:
                        for u in range(UNITS_BEFORE[s], UNITS_BEFORE[s + 1]):
                            output_unit(p, other, u)
                    if s < LAG and not first:
                        x_kT(p - 1, STEPS - LAG + s)
                    elif s >= LAG and not tail:
                        x_kT(p, s - LAG)
                    if not tail and s == 1:
                        pe.wait_ge(s_stat, p * STAT + 10)
                        ring(ring_stats(p, 2), 2, [(slice(0, 2), W_raw[:, c, :], beta_mean[:, c, :], c == 0, c == CC - 1)
                                                for c in range(CC)])
                        pe.wait_ge(s_stat, p * STAT + 11)
                        ring(ring_stats(p, 3), 3, [(slice(0, P), ones[D:P, :], ksum_rows[D:P, :], True, True)])

            periods(pe, period)

        @block.vector
        def _(dve):
            dve.wait_ge(s_const, 2)
            for h in range(2):
                nc.vector.tensor_tensor(fold_halves[:, h * D:(h + 1) * D], identity[:, 0:D], identity[:, D:P],
                                        ALU.add)
            dve.wait_ge(s_wt, 1)
            nc.vector.tensor_copy(W_raw[:, :, :].rearrange("p c j -> p (c j)"), ps_xT[0][:, :]).then_inc(s_wc, 1)
            for c in range(CC):
                dve.wait_ge(s_wt, c + 2)
                nc.vector.tensor_copy(WvT[:, c, :], ps_xT[(c + 1) % 2][:, :]).then_inc(s_wc, 1)

            def tile_stats(p, buffer, t):
                dve.wait_ge(s_x[buffer][t], (p - buffer + 2) * 8)
                for c in range(CC):
                    nc.vector.bn_stats(bn[:, c, t, :], X[buffer][:, c, t * TN:(t + 1) * TN]).then_inc(s_bn, 1)

            def taken(number, k):
                dve.wait_ge(s_ring, number + 1)
                return ps_ring[k % 2]

            def chain(ins, value):
                ins.then_inc(s_stat, 1)
                dve.wait_ge(s_stat, value)

            def means(p):
                dve.wait_ge(s_bn, (p + 1) * TILES * CC)
                settle(dve)
                for c in range(CC):
                    last = nc.vector.bn_aggr(mv[:, c, :], bn[:, c, :, :].rearrange("p t k -> p (t k)"))
                chain(last, p * STAT + 1)

            def variances(p, parity):
                bank = taken(ring_stats(p, 0), 0)
                nc.vector.tensor_scalar(neg_mean[parity][:, :], bank[:, 0:CC], -1.0, None, ALU.mult)\
                    .then_inc(s_free, 1)
                dve.wait_ge(s_free, ring_stats(p, 0) + 1)
                chain(nc.vector.tensor_tensor(dev[:, :], mv[:, :, 0], neg_mean[parity][:, :], ALU.add),
                      p * STAT + 2)
                chain(nc.vector.tensor_tensor(r0[:, :], dev[:, :], dev[:, :], ALU.mult), p * STAT + 3)
                nc.vector.tensor_tensor(e2[:, :], r0[:, :], mv[:, :, 1], ALU.add).then_inc(s_stat, 1)

            def scales(p, parity):
                bank = taken(ring_stats(p, 1), 1)
                nc.vector.tensor_scalar(gvar[:, :], bank[:, 0:CC], EPS, None, ALU.add).then_inc(s_free, 1)
                dve.wait_ge(s_root, p + 1)
                a, a1 = scale_a[parity][:, :], scale_a1[parity][:, :]
                chain(nc.vector.reciprocal(r0[:, :], root[:, :]), p * STAT + 5)
                chain(nc.vector.tensor_tensor(r1[:, :], r0[:, :], r0[:, :], ALU.mult), p * STAT + 6)
                chain(nc.vector.tensor_tensor(r1[:, :], r1[:, :], gvar[:, :], ALU.mult), p * STAT + 7)
                chain(nc.vector.tensor_scalar(r1[:, :], r1[:, :], -0.5, 1.5, ALU.mult, ALU.add), p * STAT + 8)
                chain(nc.vector.tensor_tensor(a, r0[:, :], r1[:, :], ALU.mult), p * STAT + 9)
                nc.vector.tensor_tensor(beta[parity][:, :], a, neg_mean[parity][:, :], ALU.mult)
                nc.vector.tensor_tensor(beta_mean[:, :, 0], a, neg_mean[parity][:, :], ALU.mult)
                nc.vector.tensor_tensor(beta_mean[:, :, 1], a, dev[:, :], ALU.mult)
                nc.vector.tensor_scalar(a1, a, 1.0, None, ALU.add).then_inc(s_stat, 1)

            def biases(p, parity):
                bank = taken(ring_stats(p, 2), 2)
                nc.vector.tensor_tensor(b_fold[parity][:, :], bank[:, 0:1], b_raw[:, :], ALU.add)
                nc.vector.tensor_tensor(kmean[:, :], bank[:, 1:2], b_raw[:, :], ALU.add).then_inc(s_free, 1)
                dve.wait_ge(s_free, ring_stats(p, 2) + 1)
                nc.vector.tensor_scalar(ksum_rows[:, :], fold_halves[:, :], kmean[:, :], float(N), ALU.mult,
                                        ALU.mult).then_inc(s_stat, 1)
                bank = taken(ring_stats(p, 3), 3)
                nc.vector.tensor_copy(ksum_all[parity][:, :], bank[:, 0:P]).then_inc(s_free, 1)

            def q_low(p, parity, t):
                q = slice(t * TN, (t + 1) * TN)
                dve.wait_ge(s_qhi, tile_no(p, t) + 1)
                nc.vector.scalar_tensor_tensor(out=q_hl[parity][D:P, q], in0=ps_qk[t % 2][0:D, :],
                                               scalar=b_fold[parity][0:D, :],
                                               in1=q_hl[parity][0:D, q].bitcast(f32),
                                               op0=ALU.add, op1=ALU.subtract).then_inc(s_qlo, 1)

            def kT_low(p, t):
                dve.wait_ge(s_kThi, tile_no(p, t) + 1)
                nc.vector.tensor_tensor(kT_hl[t % 2][:, :, D:P],
                                        ps_kT[:, 0:CHUNKS * D].rearrange("p (j d) -> p j d", d=D),
                                        kT_hl[t % 2][:, :, 0:D].bitcast(f32), ALU.subtract).then_inc(s_kTlo, 1)

            def xT_low(p, s):
                j = s % CHUNKS
                dve.wait_ge(s_xThi, step_no(p, s) + 1)
                nc.vector.tensor_tensor(xT_lo[:, j, :], ps_xT[s % 2][:, :], xT_hi[:, j, :].bitcast(f32),
                                        ALU.subtract).then_inc(s_xTlo, 1)

            def gather_sum(p):
                dve.wait_ge(s_S, p * STEPS)
                nc.vector.tensor_copy(ST[:, :], ps_S[:, :]).then_inc(s_sum, 1)

            def normalise_sum(p, other):
                bank = taken(ring_small(p, 0), 0)
                for c in range(CC):
                    last = nc.vector.scalar_tensor_tensor(out=SC[:, c, :], in0=ksum_all[other][:, :],
                                                          scalar=neg_mean[other][:, c:c + 1],
                                                          in1=bank[:, c * P:(c + 1) * P],
                                                          op0=ALU.mult, op1=ALU.add)
                last.then_inc(s_free, 1)
                dve.wait_ge(s_free, ring_small(p, 0) + 1)
                for c in range(CC):
                    last = nc.vector.tensor_scalar(SC[:, c, :], SC[:, c, :], scale_a[other][:, c:c + 1], None,
                                                   ALU.mult)
                last.then_inc(s_sum, 1)

            def split_vk(p):
                bank = taken(ring_small(p, 1), 1)
                nc.vector.tensor_scalar(VK_hi[:, :], bank[:, :], gamma_col[:, :], None, ALU.mult)\
                    .then_inc(s_sum, 1)
                dve.wait_ge(s_sum, p * SMALL)
                nc.vector.scalar_tensor_tensor(out=VK_lo[:, :], in0=bank[:, :], scalar=gamma_col[:, :],
                                               in1=VK_hi[:, :].bitcast(f32), op0=ALU.mult, op1=ALU.subtract)\
                    .then_inc(s_free, 1)

            def result(p, other, u):
                t, c = u // CC, u % CC
                bank = taken(ring_out(p, u), u)
                dve.wait_ge(s_res, ((p - 1) * TILES + t) * CC + c + 1)
                y = X[other][:, c, t * TN:(t + 1) * TN]
                nc.vector.tensor_tensor(y, bank[:, :], y, ALU.add).then_inc(s_free, 1)

            def period(p, parity):
                tail = is_int(p) and p == IMAGES
                first = is_int(p) and p == 0
                last = is_int(p) and p == IMAGES - 1
                other = 1 - parity
                for s in range(STEPS):
                    t, j = s // CHUNKS, s % CHUNKS
                    if s == 0:
                        if not tail:
                            means(p)
                        if not first:
                            q_low(p - 1, other, TILES - 1)
                        if not tail:
                            variances(p, parity)
                        if not first:
                            kT_low(p - 1, TILES - 1)
                        if not tail:
                            scales(p, parity)
                    elif j == 0 and not tail:
                        q_low(p, parity, t - 1)
                        kT_low(p, t - 1)
                    if not first:
                        if s == STEP_SUM:
                            gather_sum(p)
                        if s == STEP_J:
                            normalise_sum(p, other)
                        if s == STEP_VK:
                            split_vk(p)
                        for u in range(UNITS_BEFORE[s], UNITS_BEFORE[s + 1]):
                            result(p, other, u)
                    if not tail:
                        xT_low(p, s)
                        if s == 1:
                            biases(p, parity)
                        if not last:
                            for tt in STATS_AT.get(s, []):
                                tile_stats(p + 1, other, tt)

            dve.wait_ge(s_weights, 16 * 7)
            for t in range(TILES):
                tile_stats(0, 0, t)
            periods(dve, period)


_INS = ['x', 'L0_conv_Wq', 'L0_conv_bq', 'L0_conv_Wk', 'L0_conv_bk', 'L0_conv_Wv', 'L0_conv_bv', 'L0_conv_gamma']


def kernel(**inputs):
    import numpy as _np
    import concourse.bacc as _bacc
    from concourse import mybir as _mybir
    from concourse.bass_utils import run_bass_kernel_spmd as _run

    nc = _bacc.Bacc("TRN2", target_bir_lowering=False, num_devices=1)
    arrays, args = {}, []
    for name in _INS:
        a = _np.ascontiguousarray(inputs[name])
        arrays[f"in_{name}_dram"] = a
        args.append(nc.dram_tensor(f"in_{name}_dram", a.shape, _mybir.dt.from_np(a.dtype), kind="ExternalInput").ap())
    shape, dtype = inputs['x'].shape, _mybir.dt.from_np(_np.dtype('float32'))
    args.append(nc.dram_tensor("out_0_dram", shape, dtype, kind="ExternalOutput").ap())
    bass_groupnorm_linear_attention(nc, *args)
    r = _run(nc, [arrays], core_ids=[0])
    return r.results[0]["out_0_dram"]
```

```python
import concourse.bass as bass
from concourse import mybir
from contextlib import ExitStack


def bass_groupnorm_linear_attention(
    nc: bass.Bass,
    x: bass.AP,
    Wq: bass.AP,
    bq: bass.AP,
    Wk: bass.AP,
    bk: bass.AP,
    Wv: bass.AP,
    bv: bass.AP,
    gamma: bass.AP,
    out: bass.AP,
):
    f32, f32r = mybir.dt.float32, mybir.dt.float32r
    ALU = mybir.AluOpType
    ACT = mybir.ActivationFunctionType

    P = 128
    IMAGES, C, HEIGHT, WIDTH = x.shape
    N = HEIGHT * WIDTH
    D = Wq.shape[0]
    CC = C // P
    TN = 512
    TILES = N // TN
    CHUNKS = TN // P
    STEPS = TILES * CHUNKS
    GROUP = C // 32
    EPS = 1e-5
    Q_OWN = 4
    LAG = CHUNKS
    assert 2 * D == P and CC == CHUNKS and IMAGES % 2 == 0

    STEP_SUM = LAG // 2
    STEP_J = STEP_SUM + 1
    STEP_VK = STEP_SUM + 2
    STEP_OUT = STEP_SUM + 3
    UNITS = TILES * CC
    PART = 2
    PARTS = UNITS // PART
    LOAD_LAG = 2
    UNITS_AT = [0] * STEPS
    left = UNITS
    for s in range(STEP_OUT, STEPS):
        UNITS_AT[s] = min(2, left)
        left -= UNITS_AT[s]
    UNITS_BEFORE = [sum(UNITS_AT[:s]) for s in range(STEPS + 1)]
    PROJECT_AT = [[] for _ in range(STEPS)]
    for n in range(UNITS):
        PROJECT_AT[max(n // 2, n - 2)].append((n // CC, n % CC))
    TILE_OUT_AT = {}
    for s in range(STEPS):
        for t, c in PROJECT_AT[s]:
            if c == CC - 1:
                TILE_OUT_AT[s + 1] = t
    SUM_AT = [[2 * s - LAG, 2 * s - LAG + 1] if s < LAG // 2 else [s - LAG] if s >= LAG else []
              for s in range(STEPS)]
    STEP_STATS = STEP_OUT + 5
    STEP_SCALE = STEPS - 4
    STEP_KSUM = 2 * CHUNKS
    KSUM_TILES = sum(s <= STEP_KSUM for s in TILE_OUT_AT)
    STAT_PRODUCTS = 4
    STATS_AT = [[] for _ in range(STEPS)]
    for n in range(TILES * CC):
        STATS_AT[STEP_STATS + n * (STEP_SCALE - STEP_STATS) // UNITS].append((n // CC, n % CC))

    first_left = STEP_SCALE - CC
    RESIDUAL_AT = [[s - CC] if CC <= s < STEP_SCALE else [] for s in range(STEPS)]
    for n in range(first_left, UNITS):
        RESIDUAL_AT[(n - first_left) // 2].append(n - UNITS)

    BY_DVE, BY_POOL = range(2)
    POOL_TOO = [3 * CHUNKS, 4 * CHUNKS]
    LOW_BY = [BY_POOL if s % 2 or s in POOL_TOO else BY_DVE for s in range(STEPS)]

    RING_SMALL = 2
    RING = RING_SMALL + UNITS

    x_v = x.rearrange("b (c p) h w -> b p c (h w)", p=P)
    out_v = out.rearrange("b (c p) h w -> b p c (h w)", p=P)

    ctx = ExitStack()
    with ctx:
        def sb(name, shape, dt=f32):
            return ctx.enter_context(nc.sbuf_tensor(name, shape, dt))

        def pb(name, shape, dt=f32):
            return ctx.enter_context(nc.psum_tensor(name, shape, dt))

        def sem(name):
            return ctx.enter_context(nc.semaphore(name))

        X = [sb(f"X{i}", [P, CC, N]) for i in range(2)]
        q_own = [sb(f"q_own{i}", [P, Q_OWN, TN], f32r) for i in range(2)]
        q_shared = sb("q_shared", [P, TILES - Q_OWN, TN], f32r)
        xT_hi = sb("xT_hi", [P, CHUNKS, C], f32r)
        xT_lo = sb("xT_lo", [P, CHUNKS, C], f32r)
        xT_whole = sb("xT_whole", [P, C])
        kT_hl = [sb(f"kT_hl{i}", [P, CHUNKS, P], f32r) for i in range(2)]
        k_row = sb("k_row", [P, TN])
        k_nat = k_row[D:P, :]
        bv_row = k_row[0:1, 0:C]
        W_raw = sb("W_raw", [P, CC, P])
        W_fold = [sb(f"W_fold{i}", [P, CC, P]) for i in range(2)]
        WvT = sb("WvT", [P, CC, C])
        ST = sb("ST", [P, C])
        ksum_beta = sb("ksum_beta", [P, CC, P])
        SC = ST[:, :].rearrange("p (c j) -> p c j", j=P)
        VK_hi = sb("VK_hi", [P, C], f32r)
        VK_lo = sb("VK_lo", [P, C], f32r)
        identity = sb("identity", [P, P])
        fold_halves = sb("fold_halves", [P, P])
        group_mean = sb("group_mean", [P, P])
        all_n = sb("all_n", [P, P])
        bn = sb("bn", [P, CC, TILES, 6])
        mv = sb("mv", [P, CC, 2])
        dev = sb("dev", [P, CC])
        e2 = sb("e2", [P, CC])
        gvar = sb("gvar", [P, CC])
        dev2 = sb("dev2", [P, CC])
        minus_half = sb("minus_half", [P, CC])
        beta_mean = sb("beta_mean", [P, CC, 2])
        b_raw = sb("b_raw", [P, 1])
        gamma_col = sb("gamma_col", [P, 1])
        kmean = sb("kmean", [P, 1])
        ksum_rows = sb("ksum_rows", [P, P])
        neg_mean = [sb(f"neg_mean{i}", [P, CC]) for i in range(2)]
        scale_a = [sb(f"scale_a{i}", [P, CC]) for i in range(2)]
        scale_a1 = [sb(f"scale_a1{i}", [P, CC]) for i in range(2)]
        beta = [sb(f"beta{i}", [P, CC]) for i in range(2)]
        b_fold = [sb(f"b_fold{i}", [P, 1]) for i in range(2)]
        ksum_all = [sb(f"ksum_all{i}", [P, P]) for i in range(2)]

        Wv_nat = X[1][:, 0, 0:CC * C].rearrange("p (o c) -> p o c", c=C)
        W_nat = X[1][:, 1, 0:C]

        ps_qk = [pb(f"ps_qk{i}", [P, TN]) for i in range(2)]
        ps_xT = [pb(f"ps_xT{i}", [P, C]) for i in range(2)]
        ps_kT = pb("ps_kT", [P, TN])
        ps_S = pb("ps_S", [P, C])
        ps_ring = [pb(f"ps_ring{i}", [P, TN]) for i in range(2)]

        s_weights = sem("s_weights")
        s_x = [[sem(f"s_x{i}_{r}") for r in range(PARTS)] for i in range(2)]
        s_y = [sem(f"s_y{r}") for r in range(PARTS)]
        s_const0 = sem("s_const0")
        s_const = sem("s_const")
        s_wt = sem("s_wt")
        s_wc = sem("s_wc")
        s_bn = sem("s_bn")
        s_mean = sem("s_mean")
        s_stat = sem("s_stat")
        s_sprod = sem("s_sprod")
        s_taken = sem("s_taken")
        s_fold = sem("s_fold")
        s_proj = sem("s_proj")
        s_xT = sem("s_xT")
        s_kT = sem("s_kT")
        s_S = sem("s_S")
        s_k = sem("s_k")
        s_qhi = sem("s_qhi")
        s_qlo = sem("s_qlo")
        s_kThi = sem("s_kThi")
        s_kTlo = sem("s_kTlo")
        s_xThi = sem("s_xThi")
        s_xTwhole = sem("s_xTwhole")
        s_xTlo = [sem("s_xTlo_dve"), sem("s_xTlo_pool")]
        s_sum = sem("s_sum")
        s_ring = sem("s_ring")
        s_free = sem("s_free")
        s_res = sem("s_res")

        s_kb = sem("s_kb")

        s_passed = sem("s_passed")

        block = ctx.enter_context(nc.Block())

        def tile_no(p, t):
            return p * TILES + t

        def step_no(p, s):
            return p * STEPS + s

        def settle(eng):
            eng.sem_inc(s_passed, 1)

        def q_tile(parity, t):
            return q_own[parity][:, t, :] if t < Q_OWN else q_shared[:, t - Q_OWN, :]

        def low_no(p, s):
            return p * LOW_BY.count(LOW_BY[s]) + LOW_BY[:s].count(LOW_BY[s])

        def is_int(v):
            return isinstance(v, int)

        def ring_small(p, k):
            return (p - 1) * RING + k

        def ring_out(p, u):
            return ring_small(p, RING_SMALL + u)

        def ring_read(number):
            return number + 3

        STAT = 5
        SMALL = 2

        def periods(eng, period):
            period(0, 0)
            with eng.Fori(0, IMAGES // 2 - 1) as it:
                period(it * 2 + 1, 1)
                period(it * 2 + 2, 0)
            period(IMAGES - 1, 1)
            period(IMAGES, 0)

        def wait_count(eng, s, value):
            if not is_int(value) or value > 0:
                eng.wait_ge(s, value)

        @block.sync
        def _(sp):
            sp.dma_start(W_nat[0:D, :], Wq).then_inc(s_weights, 16)
            sp.dma_start(W_nat[D:P, :], Wk).then_inc(s_weights, 16)
            sp.dma_start(Wv_nat, Wv.rearrange("(o p) c -> p o c", p=P)).then_inc(s_weights, 16)
            with nc.allow_non_contiguous_dma(reason="one bias per partition"):
                sp.dma_start(b_raw[0:D, :], bq.rearrange("(p a) -> p a", a=1)).then_inc(s_weights, 16)
                sp.dma_start(b_raw[D:P, :], bk.rearrange("(p a) -> p a", a=1)).then_inc(s_weights, 16)
                sp.dma_start(gamma_col[:, :], gamma.rearrange("(a n) -> a n", a=1).to_broadcast([P, 1]))\
                    .then_inc(s_weights, 16)
            sp.dma_start(bv_row, bv.rearrange("(a n) -> a n", a=1)).then_inc(s_weights, 16)

            def part(array, r):
                t, c = r * PART // CC, r * PART % CC
                return array[:, c:c + PART, t * TN:(t + 1) * TN]

            def load(p, buffer, r):
                sp.dma_start(part(X[buffer], r), part(x_v[p], r)).then_inc(s_x[buffer][r], 16)

            for r in range(PARTS):
                load(0, 0, r)
            sp.wait_ge(s_wc, CC + 1)
            for r in range(PARTS):
                load(1, 1, r)

            def period(p, parity):
                if is_int(p) and p == 0:
                    return
                other = 1 - parity
                loads = not (is_int(p) and p >= IMAGES - 1)
                for r in range(PARTS + LOAD_LAG):
                    if r < PARTS:
                        sp.wait_ge(s_free, ring_read(ring_out(p, (r + 1) * PART - 1)))
                        sp.dma_start(part(out_v[p - 1], r), part(X[other], r)).then_inc(s_y[r], 16)
                    if loads and r >= LOAD_LAG:
                        sp.wait_ge(s_y[r - LOAD_LAG], p * 16)
                        load(p + 1, other, r - LOAD_LAG)

            periods(sp, period)
            for r in range(PARTS):
                sp.wait_ge(s_y[r], IMAGES * 16)

        @block.gpsimd
        def _(pool):
            nc.gpsimd.memset(identity[:, :], 0.0).then_inc(s_const0, 1)
            nc.gpsimd.memset(group_mean[:, :], 1.0 / GROUP).then_inc(s_const0, 1)
            nc.gpsimd.memset(all_n[:, :], float(N)).then_inc(s_const0, 1)
            nc.gpsimd.memset(minus_half[:, :], -0.5).then_inc(s_const0, 1)
            pool.wait_ge(s_const0, 4)
            nc.gpsimd.affine_select(out=identity[:, :], in_=identity[:, :], compare_op=ALU.not_equal, fill=1.0,
                                    base=0, pattern=[[-1, P]], channel_multiplier=1).then_inc(s_const, 1)
            gm = group_mean[:, :].rearrange("p (g c) -> p g c", c=GROUP)
            nc.gpsimd.affine_select(out=gm, in_=gm, compare_op=ALU.is_ge, fill=0.0, base=0,
                                    pattern=[[-GROUP, P // GROUP], [0, GROUP]], channel_multiplier=1)\
                .then_inc(s_const0, 1)
            pool.wait_ge(s_const0, 5)
            nc.gpsimd.affine_select(out=gm, in_=gm, compare_op=ALU.is_ge, fill=0.0, base=GROUP - 1,
                                    pattern=[[GROUP, P // GROUP], [0, GROUP]], channel_multiplier=-1)\
                .then_inc(s_const, 1)

            def chain(ins, value):
                ins.then_inc(s_stat, 1)
                pool.wait_ge(s_stat, value)
                settle(pool)

            def deviations(p, parity):
                pool.wait_ge(s_taken, p * STAT + 1)
                chain(nc.gpsimd.tensor_tensor(dev[:, :], mv[:, :, 0], neg_mean[parity][:, :], ALU.add), p * STAT + 1)
                chain(nc.gpsimd.tensor_tensor(dev2[:, :], dev[:, :], dev[:, :], ALU.mult), p * STAT + 2)
                nc.gpsimd.tensor_tensor(e2[:, :], dev2[:, :], mv[:, :, 1], ALU.add).then_inc(s_stat, 1)

            def scales(p, parity):
                a = scale_a[parity][:, :]
                pool.wait_ge(s_taken, p * STAT + 2)
                chain(nc.gpsimd.tensor_tensor(a, gvar[:, :], minus_half[:, :], ALU.pow), p * STAT + 4)
                for c in range(CC):
                    nc.gpsimd.tensor_scalar(W_fold[parity][:, c, :], W_raw[:, c, :], scale_a[parity][:, c:c + 1],
                                            1.0, ALU.mult, ALU.mult).then_inc(s_fold, 1)
                nc.gpsimd.tensor_tensor(beta[parity][:, :], a, neg_mean[parity][:, :], ALU.mult)
                nc.gpsimd.tensor_tensor(beta_mean[:, :, 0], a, neg_mean[parity][:, :], ALU.mult)
                nc.gpsimd.tensor_tensor(beta_mean[:, :, 1], a, dev[:, :], ALU.mult)
                chain(nc.gpsimd.tensor_scalar(scale_a1[parity][:, :], a, 1.0, 1.0, ALU.mult, ALU.add),
                      p * STAT + 5)

            def residual(p, parity, t, c):
                if c == 0:
                    pool.wait_ge(s_proj, tile_no(p, t) + 1)
                    pool.wait_ge(s_xT, step_no(p, (t + 1) * CHUNKS))
                    settle(pool)
                xs = X[parity][:, c, t * TN:(t + 1) * TN]
                nc.gpsimd.tensor_scalar(xs, xs, scale_a1[parity][:, c:c + 1], beta[parity][:, c:c + 1],
                                        ALU.mult, ALU.add).then_inc(s_res, 1)

            def products_ksum_beta(p, parity):
                pool.wait_ge(s_taken, p * STAT + 5)
                if not (is_int(p) and p == 0):
                    pool.wait_ge(s_free, ring_read(ring_small(p, 0)))
                settle(pool)
                for c in range(CC):
                    nc.gpsimd.tensor_scalar(ksum_beta[:, c, :], ksum_all[parity][:, :], beta[parity][:, c:c + 1],
                                            1.0, ALU.mult, ALU.mult).then_inc(s_kb, 1)

            def xT_low(p, s):
                pool.wait_ge(s_xTwhole, low_no(p, s) + 1)
                j = s % CHUNKS
                nc.gpsimd.tensor_tensor(xT_lo[:, j, :], xT_whole[:, :], xT_hi[:, j, :].bitcast(f32),
                                        ALU.subtract).then_inc(s_xTlo[BY_POOL], 1)

            def period(p, parity):
                if is_int(p) and p == IMAGES:
                    for n in [n for at in RESIDUAL_AT for n in at if n < 0]:
                        residual(p - 1, 1 - parity, TILES + n // CC, n % CC)
                    return
                for s in range(STEPS):
                    if not (is_int(p) and p == IMAGES - 1):
                        if s == STEP_SCALE + 1:
                            deviations(p + 1, 1 - parity)
                        if s == STEP_SCALE + 2:
                            scales(p + 1, 1 - parity)
                    if s == STEP_KSUM + 4:
                        products_ksum_beta(p, parity)
                    for n in RESIDUAL_AT[s]:
                        if n >= 0:
                            residual(p, parity, n // CC, n % CC)
                        elif not (is_int(p) and p == 0):
                            residual(p - 1, 1 - parity, TILES + n // CC, n % CC)
                    if LOW_BY[s] == BY_POOL:
                        xT_low(p, s)

            pool.wait_ge(s_wc, 1)
            deviations(0, 0)
            scales(0, 0)
            periods(pool, period)

        @block.scalar
        def _(act):
            act.wait_ge(s_weights, 16 * 7)

            def k_out(p, parity, t):
                n = tile_no(p, t)
                if t == 0:
                    act.wait_ge(s_taken, p * STAT + 3)
                act.wait_ge(s_proj, n + 1)
                wait_count(act, s_kT, n)
                nc.scalar.activation(k_nat, ps_qk[t % 2][D:P, :], ACT.Identity, bias=b_fold[parity][D:P, :]).then_inc(s_k, 1)

            def q_high(p, parity, t):
                if t >= Q_OWN and not (is_int(p) and p == 0):
                    act.wait_ge(s_ring, ring_out(p, (t + 1) * CC))
                nc.scalar.activation(q_tile(parity, t)[0:D, :], ps_qk[t % 2][0:D, :], ACT.Identity,
                                     bias=b_fold[parity][0:D, :]).then_inc(s_qhi, 1)

            def kT_high(p, t):
                n = tile_no(p, t)
                act.wait_ge(s_kT, n + 1)
                wait_count(act, s_S, (n - 1) * CHUNKS)
                nc.scalar.activation(kT_hl[t % 2][:, :, 0:D], ps_kT[:, 0:CHUNKS * D].rearrange("p (j d) -> p j d", d=D),
                                     ACT.Copy).then_inc(s_kThi, 1)

            def xT_high(p, s):
                g = step_no(p, s)
                act.wait_ge(s_xT, g + 1)
                wait_count(act, s_S, g - LAG + 1)
                nc.scalar.activation(xT_hi[:, s % CHUNKS, :], ps_xT[s % 2][:, :], ACT.Copy).then_inc(s_xThi, 1)

            def xT_for_pool(p, s):
                if LOW_BY[s] == BY_POOL:
                    wait_count(act, s_xTlo[BY_POOL], low_no(p, s))
                    nc.scalar.activation(xT_whole[:, :], ps_xT[s % 2][:, :], ACT.Copy).then_inc(s_xTwhole, 1)

            def statistics_taken(p, parity, k):
                act.wait_ge(s_sprod, p * STAT_PRODUCTS + k + 1)
                if k == 0:
                    nc.scalar.activation(neg_mean[parity][:, :], ps_ring[0][:, 0:CC], ACT.Copy, scale=-1.0)\
                        .then_inc(s_taken, 1)
                if k == 1:
                    nc.scalar.activation(gvar[:, :], ps_ring[1][:, 0:CC], ACT.Copy, bias=EPS).then_inc(s_taken, 1)
                if k == 2:
                    nc.scalar.activation(b_fold[parity][:, :], ps_ring[0][:, 0:1], ACT.Identity, bias=b_raw[:, :])
                    nc.scalar.activation(kmean[:, :], ps_ring[0][:, 1:2], ACT.Identity, bias=b_raw[:, :])\
                        .then_inc(s_taken, 1)
                    act.wait_ge(s_taken, p * STAT + 3)
                    nc.scalar.activation(ksum_rows[:, :], fold_halves[:, :], ACT.Copy, scale=kmean[:, :])\
                        .then_inc(s_taken, 1)
                if k == 3:
                    nc.scalar.activation(ksum_all[parity][:, :], ps_kT[:, 0:P], ACT.Copy).then_inc(s_taken, 1)

            def period(p, parity):
                tail = is_int(p) and p == IMAGES
                last = is_int(p) and p == IMAGES - 1
                for s in range(0 if tail else STEPS):
                    if s + 1 in TILE_OUT_AT:
                        k_out(p, parity, TILE_OUT_AT[s + 1])
                    if s == STEP_SCALE + 1 and not last:
                        statistics_taken(p + 1, 1 - parity, 0)
                    if s in TILE_OUT_AT:
                        kT_high(p, TILE_OUT_AT[s])
                    xT_high(p, s)
                    if s + 1 in TILE_OUT_AT:
                        q_high(p, parity, TILE_OUT_AT[s + 1])
                    if s == STEP_SCALE + 2 and not last:
                        statistics_taken(p + 1, 1 - parity, 1)
                    xT_for_pool(p, s)
                    if s == 0:
                        statistics_taken(p, parity, 2)
                    if s == STEP_KSUM:
                        statistics_taken(p, parity, 3)

            for k in range(2):
                statistics_taken(0, 0, k)
            periods(act, period)

        @block.tensor
        def _(pe):
            pe.wait_ge(s_const, 2)
            pe.wait_ge(s_weights, 16 * 7)
            for c in range(CC):
                last = nc.tensor.transpose(ps_xT[0][:, c * P:(c + 1) * P], W_nat[:, c * P:(c + 1) * P],
                                           identity[:, :])
            last.then_inc(s_wt, 1)
            for c in range(CC):
                wait_count(pe, s_wc, c)
                for o in range(CC):
                    last = nc.tensor.transpose(ps_xT[(c + 1) % 2][:, o * P:(o + 1) * P],
                                               Wv_nat[:, o, c * P:(c + 1) * P], identity[:, :])
                last.then_inc(s_wt, 1)
            pe.wait_ge(s_wc, CC + 1)

            def project(p, parity, t, c):
                if c == 0:
                    n = tile_no(p, t)
                    wait_count(pe, s_k, n - 1)
                    wait_count(pe, s_qlo, n - 1)
                if t == 0:
                    pe.wait_ge(s_fold, p * CC + c + 1)
                mm = nc.tensor.matmul(ps_qk[t % 2][:, :], W_fold[parity][:, c, :],
                                      X[parity][:, c, t * TN:(t + 1) * TN], start=(c == 0), stop=(c == CC - 1))
                if c == CC - 1:
                    mm.then_inc(s_proj, 1)

            def transpose_x(p, parity, s):
                if s >= 2 or not (is_int(p) and p == 0):
                    before = (p, s - 2) if s >= 2 else (p - 1, STEPS + s - 2)
                    pe.wait_ge(s_xTwhole if LOW_BY[before[1]] == BY_POOL else s_xTlo[BY_DVE], low_no(*before) + 1)
                for c in range(CC):
                    last = nc.tensor.transpose(ps_xT[s % 2][:, c * P:(c + 1) * P],
                                               X[parity][:, c, s * P:(s + 1) * P], identity[:, :])
                last.then_inc(s_xT, 1)

            def transpose_k(p, t):
                n = tile_no(p, t)
                pe.wait_ge(s_k, n + 1)
                wait_count(pe, s_kTlo, n)
                if t == KSUM_TILES:
                    pe.wait_ge(s_taken, p * STAT + 5)
                settle(pe)
                for j in range(CHUNKS):
                    last = nc.tensor.transpose(ps_kT[:, j * D:(j + 1) * D], k_nat[:, j * P:(j + 1) * P],
                                               identity[D:P, D:P])
                last.then_inc(s_kT, 1)

            def x_kT(p, s):
                t, j = s // CHUNKS, s % CHUNKS
                if j == 0:
                    pe.wait_ge(s_kTlo, tile_no(p, t) + 1)
                if s == 0:
                    wait_count(pe, s_sum, (p - 1) * SMALL + 1)
                pe.wait_ge(s_xTlo[LOW_BY[s]], low_no(p, s) + 1)
                nc.tensor.matmul(ps_S[:, :], kT_hl[t % 2][:, j, :], xT_hi[:, j, :], start=(s == 0), stop=False)
                nc.tensor.matmul(ps_S[:, :], kT_hl[t % 2][:, j, :], xT_lo[:, j, :], start=False,
                                 stop=(s == STEPS - 1)).then_inc(s_S, 1)

            def product_j(p):
                number = ring_small(p, 0)
                pe.wait_ge(s_free, ring_read(number - 2))
                pe.wait_ge(s_sum, (p - 1) * SMALL + 1)
                for c in range(CC):
                    last = nc.tensor.matmul(ps_ring[0][:, c * P:(c + 1) * P], ST[:, c * P:(c + 1) * P],
                                            fold_halves[:, :], start=True, stop=True)
                last.then_inc(s_ring, 1)

            def product_vk(p, other):
                number = ring_small(p, 1)
                pe.wait_ge(s_free, ring_read(number - 2))
                nc.tensor.matmul(ps_ring[1][:, :], ksum_all[other][0:1, :], bv_row, start=True, stop=False)
                pe.wait_ge(s_free, ring_read(ring_small(p, 0)))
                for c in range(CC):
                    last = nc.tensor.matmul(ps_ring[1][:, :], SC[:, c, :], WvT[:, c, :], start=False,
                                            stop=(c == CC - 1))
                last.then_inc(s_ring, 1)

            def sums(p, s, first, tail):
                for step in SUM_AT[s]:
                    if step < 0 and not first:
                        x_kT(p - 1, STEPS + step)
                    if step >= 0 and not tail:
                        x_kT(p, step)

            def output_unit(p, other, u):
                t, c = u // CC, u % CC
                number = ring_out(p, u)
                if u == 0:
                    pe.wait_ge(s_qlo, p * TILES)
                    pe.wait_ge(s_sum, p * SMALL)
                pe.wait_ge(s_free, ring_read(number - 2))
                q = q_tile(other, t)
                bank = ps_ring[u % 2]
                nc.tensor.matmul(bank[:, :], VK_hi[:, c * P:(c + 1) * P], q, start=True, stop=False)
                if u == 0:
                    pe.wait_ge(s_free, ring_read(ring_small(p, 1)))
                nc.tensor.matmul(bank[:, :], VK_lo[:, c * P:(c + 1) * P], q, start=False, stop=True)\
                    .then_inc(s_ring, 1)

            def statistics_product(p, k):
                bank = ps_ring[k % 2] if k < 3 else ps_kT
                if k == 0:
                    if not (is_int(p) and p <= 1):
                        pe.wait_ge(s_free, ring_read(ring_small(p, 0) - 1))
                    pe.wait_ge(s_mean, p + 1)
                    last = nc.tensor.matmul(bank[:, 0:CC], group_mean[:, :], mv[:, :, 0], start=True, stop=True)
                if k == 1:
                    pe.wait_ge(s_stat, p * STAT + 3)
                    last = nc.tensor.matmul(bank[:, 0:CC], group_mean[:, :], e2[:, :], start=True, stop=True)
                if k == 2:
                    pe.wait_ge(s_stat, p * STAT + 5)
                    for c in range(CC):
                        last = nc.tensor.matmul(bank[:, 0:2], W_raw[:, c, :], beta_mean[:, c, :],
                                                start=(c == 0), stop=(c == CC - 1))
                if k == 3:
                    wait_count(pe, s_kTlo, tile_no(p, KSUM_TILES))
                    pe.wait_ge(s_taken, p * STAT + 4)
                    last = nc.tensor.matmul(bank[:, 0:P], all_n[D:P, :], ksum_rows[D:P, :], start=True, stop=True)
                last.then_inc(s_sprod, 1)

            def period(p, parity):
                tail = is_int(p) and p == IMAGES
                first = is_int(p) and p == 0
                last = is_int(p) and p == IMAGES - 1
                other = 1 - parity
                for s in range(STEPS):
                    if s == 0:
                        sums(p, s, first, tail)
                        if not tail:
                            transpose_x(p, parity, s)
                    if not tail:
                        for tile, chunk in PROJECT_AT[s]:
                            project(p, parity, tile, chunk)
                        if s == STEP_SCALE + 1 and not last:
                            statistics_product(p + 1, 0)
                        if s > 0:
                            transpose_x(p, parity, s)
                        if s == STEP_SCALE + 2 and not last:
                            statistics_product(p + 1, 1)
                    if s == STEP_J and not first:
                        if not tail:
                            pe.wait_ge(s_taken, p * STAT + 3)
                            settle(pe)
                        product_j(p)
                    if s == STEP_VK and not first:
                        product_vk(p, other)
                    if not first:
                        for u in range(UNITS_BEFORE[s], UNITS_BEFORE[s + 1])[:1]:
                            output_unit(p, other, u)
                    if not tail and s in TILE_OUT_AT:
                        transpose_k(p, TILE_OUT_AT[s])
                    if s > 0:
                        sums(p, s, first, tail)
                    if not first:
                        for u in range(UNITS_BEFORE[s], UNITS_BEFORE[s + 1])[1:]:
                            output_unit(p, other, u)
                    if not tail and s == 0:
                        statistics_product(p, 2)
                    if not tail and s == STEP_KSUM:
                        statistics_product(p, 3)

            for k in range(2):
                statistics_product(0, k)
            periods(pe, period)

        @block.vector
        def _(dve):
            dve.wait_ge(s_const, 2)
            for h in range(2):
                nc.vector.tensor_tensor(fold_halves[:, h * D:(h + 1) * D], identity[:, 0:D], identity[:, D:P],
                                        ALU.add).then_inc(s_free, 1)
            dve.wait_ge(s_wt, 1)
            nc.vector.tensor_copy(W_raw[:, :, :].rearrange("p c j -> p (c j)"), ps_xT[0][:, :]).then_inc(s_wc, 1)
            for c in range(CC):
                dve.wait_ge(s_wt, c + 2)
                nc.vector.tensor_copy(WvT[:, c, :], ps_xT[(c + 1) % 2][:, :]).then_inc(s_wc, 1)

            def tile_stats(p, buffer, t, c):
                if c % PART == 0:
                    dve.wait_ge(s_x[buffer][(t * CC + c) // PART], (p - buffer + 2) * 8)
                nc.vector.bn_stats(bn[:, c, t, :], X[buffer][:, c, t * TN:(t + 1) * TN]).then_inc(s_bn, 1)

            def taken(number, k):
                dve.wait_ge(s_ring, number + 1)
                return ps_ring[k % 2]

            def means(p):
                dve.wait_ge(s_bn, (p + 1) * TILES * CC)
                settle(dve)
                for c in range(CC):
                    last = nc.vector.bn_aggr(mv[:, c, :], bn[:, c, :, :].rearrange("p t k -> p (t k)"))
                last.then_inc(s_mean, 1)

            def q_low(p, parity, t):
                q = q_tile(parity, t)
                dve.wait_ge(s_qhi, tile_no(p, t) + 1)
                nc.vector.scalar_tensor_tensor(out=q[D:P, :], in0=ps_qk[t % 2][0:D, :],
                                               scalar=b_fold[parity][0:D, :],
                                               in1=q[0:D, :].bitcast(f32),
                                               op0=ALU.add, op1=ALU.subtract).then_inc(s_qlo, 1)

            def kT_low(p, t):
                dve.wait_ge(s_kThi, tile_no(p, t) + 1)
                nc.vector.tensor_tensor(kT_hl[t % 2][:, :, D:P],
                                        ps_kT[:, 0:CHUNKS * D].rearrange("p (j d) -> p j d", d=D),
                                        kT_hl[t % 2][:, :, 0:D].bitcast(f32), ALU.subtract).then_inc(s_kTlo, 1)

            def xT_low(p, s):
                j = s % CHUNKS
                dve.wait_ge(s_xThi, step_no(p, s) + 1)
                nc.vector.tensor_tensor(xT_lo[:, j, :], ps_xT[s % 2][:, :], xT_hi[:, j, :].bitcast(f32),
                                        ALU.subtract).then_inc(s_xTlo[BY_DVE], 1)

            def gather_sum(p):
                dve.wait_ge(s_S, p * STEPS)
                nc.vector.tensor_copy(ST[:, :], ps_S[:, :]).then_inc(s_sum, 1)

            def normalise_sum(p, other):
                bank = taken(ring_small(p, 0), 0)
                dve.wait_ge(s_kb, p * CC)
                for c in range(CC):
                    last = nc.vector.scalar_tensor_tensor(out=SC[:, c, :], in0=bank[:, c * P:(c + 1) * P],
                                                          scalar=scale_a[other][:, c:c + 1],
                                                          in1=ksum_beta[:, c, :], op0=ALU.mult, op1=ALU.add)
                last.then_inc(s_free, 1)

            def split_vk(p):
                bank = taken(ring_small(p, 1), 1)
                nc.vector.tensor_scalar(VK_hi[:, :], bank[:, :], gamma_col[:, :], None, ALU.mult)\
                    .then_inc(s_sum, 1)
                dve.wait_ge(s_sum, p * SMALL)
                nc.vector.scalar_tensor_tensor(out=VK_lo[:, :], in0=bank[:, :], scalar=gamma_col[:, :],
                                               in1=VK_hi[:, :].bitcast(f32), op0=ALU.mult, op1=ALU.subtract)\
                    .then_inc(s_free, 1)

            def result(p, other, u):
                t, c = u // CC, u % CC
                bank = taken(ring_out(p, u), u)
                dve.wait_ge(s_res, ((p - 1) * TILES + t) * CC + c + 1)
                y = X[other][:, c, t * TN:(t + 1) * TN]
                nc.vector.tensor_tensor(y, bank[:, :], y, ALU.add).then_inc(s_free, 1)

            def period(p, parity):
                tail = is_int(p) and p == IMAGES
                first = is_int(p) and p == 0
                last = is_int(p) and p == IMAGES - 1
                other = 1 - parity
                for s in range(STEPS):
                    if s == STEP_SUM and not first:
                        gather_sum(p)
                    if s in TILE_OUT_AT and not tail:
                        q_low(p, parity, TILE_OUT_AT[s])
                        kT_low(p, TILE_OUT_AT[s])
                    if not first:
                        if s == STEP_J:
                            normalise_sum(p, other)
                        if s == STEP_VK:
                            split_vk(p)
                        for u in range(UNITS_BEFORE[s], UNITS_BEFORE[s + 1]):
                            result(p, other, u)
                    if not tail:
                        if LOW_BY[s] == BY_DVE:
                            xT_low(p, s)
                        if not last:
                            for tile, chunk in STATS_AT[s]:
                                tile_stats(p + 1, other, tile, chunk)
                            if s == STEP_SCALE - 1:
                                means(p + 1)

            dve.wait_ge(s_weights, 16 * 7)
            for t in range(TILES):
                for c in range(CC):
                    tile_stats(0, 0, t, c)
            means(0)
            periods(dve, period)


_INS = ['x', 'L0_conv_Wq', 'L0_conv_bq', 'L0_conv_Wk', 'L0_conv_bk', 'L0_conv_Wv', 'L0_conv_bv', 'L0_conv_gamma']


def kernel(**inputs):
    import numpy as _np
    import concourse.bacc as _bacc
    from concourse import mybir as _mybir
    from concourse.bass_utils import run_bass_kernel_spmd as _run

    nc = _bacc.Bacc("TRN2", target_bir_lowering=False, num_devices=1)
    arrays, args = {}, []
    for name in _INS:
        a = _np.ascontiguousarray(inputs[name])
        arrays[f"in_{name}_dram"] = a
        args.append(nc.dram_tensor(f"in_{name}_dram", a.shape, _mybir.dt.from_np(a.dtype), kind="ExternalInput").ap())
    shape, dtype = inputs['x'].shape, _mybir.dt.from_np(_np.dtype('float32'))
    args.append(nc.dram_tensor("out_0_dram", shape, dtype, kind="ExternalOutput").ap())
    bass_groupnorm_linear_attention(nc, *args)
    r = _run(nc, [arrays], core_ids=[0])
    return r.results[0]["out_0_dram"]
```

```python
import concourse.bass as bass
from concourse import mybir
from contextlib import ExitStack


def bass_groupnorm_linear_attention(
    nc: bass.Bass,
    x: bass.AP,
    Wq: bass.AP,
    bq: bass.AP,
    Wk: bass.AP,
    bk: bass.AP,
    Wv: bass.AP,
    bv: bass.AP,
    gamma: bass.AP,
    out: bass.AP,
):
    f32, f32r = mybir.dt.float32, mybir.dt.float32r
    ALU = mybir.AluOpType
    ACT = mybir.ActivationFunctionType

    P = 128
    IMAGES, C, HEIGHT, WIDTH = x.shape
    N = HEIGHT * WIDTH
    D = Wq.shape[0]
    CC = C // P
    TN = 512
    TILES = N // TN
    CHUNKS = TN // P
    STEPS = TILES * CHUNKS
    GROUP = C // 32
    EPS = 1e-5
    Q_OWN = 4
    LAG = CHUNKS
    assert 2 * D == P and CC == CHUNKS and IMAGES % 2 == 0

    STEP_SUM = LAG // 2
    STEP_J = STEP_SUM + 1
    STEP_VK = STEP_SUM + 2
    STEP_OUT = STEP_SUM + 3
    UNITS = TILES * CC
    PART = 2
    PARTS = UNITS // PART
    LOAD_LAG = 2
    UNITS_AT = [0] * STEPS
    left = UNITS
    for s in range(STEP_OUT, STEPS):
        UNITS_AT[s] = min(2, left)
        left -= UNITS_AT[s]
    UNITS_BEFORE = [sum(UNITS_AT[:s]) for s in range(STEPS + 1)]
    PROJECT_AT = [[] for _ in range(STEPS)]
    for n in range(UNITS):
        PROJECT_AT[max(n // 2, n - 2)].append((n // CC, n % CC))
    TILE_OUT_AT = {}
    for s in range(STEPS):
        for t, c in PROJECT_AT[s]:
            if c == CC - 1:
                TILE_OUT_AT[s + 1] = t
    SUM_AT = [[2 * s - LAG, 2 * s - LAG + 1] if s < LAG // 2 else [s - LAG] if s >= LAG else []
              for s in range(STEPS)]
    STEP_STATS = STEP_OUT + 5
    STEP_SCALE = STEPS - 4
    WV_AT = {c + 1: c for c in range(CC)}
    STEP_KSUM = 2 * CHUNKS
    KSUM_TILES = sum(s <= STEP_KSUM for s in TILE_OUT_AT)
    STAT_PRODUCTS = 4
    STATS_AT = [[] for _ in range(STEPS)]
    for n in range(TILES * CC):
        STATS_AT[STEP_STATS + n * (STEP_SCALE - STEP_STATS) // UNITS].append((n // CC, n % CC))

    first_left = STEP_SCALE - CC
    RESIDUAL_AT = [[s - CC] if CC <= s < STEP_SCALE else [] for s in range(STEPS)]
    for n in range(first_left, UNITS):
        RESIDUAL_AT[(n - first_left) // 2].append(n - UNITS)

    BY_DVE, BY_POOL = range(2)
    POOL_TOO = [3 * CHUNKS, 4 * CHUNKS]
    DVE_TOO = [1, STEP_SCALE + 1, STEP_SCALE + 3]
    LOW_BY = [BY_POOL if s % 2 and s not in DVE_TOO or s in POOL_TOO else BY_DVE for s in range(STEPS)]

    RING_SMALL = 2
    RING = RING_SMALL + UNITS

    x_v = x.rearrange("b (c p) h w -> b p c (h w)", p=P)
    out_v = out.rearrange("b (c p) h w -> b p c (h w)", p=P)

    ctx = ExitStack()
    with ctx:
        def sb(name, shape, dt=f32):
            return ctx.enter_context(nc.sbuf_tensor(name, shape, dt))

        def pb(name, shape, dt=f32):
            return ctx.enter_context(nc.psum_tensor(name, shape, dt))

        def sem(name):
            return ctx.enter_context(nc.semaphore(name))

        X = [sb(f"X{i}", [P, CC, N]) for i in range(2)]
        q_own = [sb(f"q_own{i}", [P, Q_OWN, TN], f32r) for i in range(2)]
        q_shared = sb("q_shared", [P, TILES - Q_OWN, TN], f32r)
        xT_hi = sb("xT_hi", [P, CHUNKS, C], f32r)
        xT_lo = sb("xT_lo", [P, CHUNKS, C], f32r)
        xT_whole = sb("xT_whole", [P, C])
        kT_hl = [sb(f"kT_hl{i}", [P, CHUNKS, P], f32r) for i in range(2)]
        k_row = sb("k_row", [P, TN])
        k_nat = k_row[D:P, :]
        W_raw = sb("W_raw", [P, CC, P])
        W_fold = [sb(f"W_fold{i}", [P, CC, P]) for i in range(2)]
        WvT = sb("WvT", [P, CC, C])
        ST = sb("ST", [P, C])
        ksum_beta = sb("ksum_beta", [P, CC, P])
        SC = ST[:, :].rearrange("p (c j) -> p c j", j=P)
        VK_hi = sb("VK_hi", [P, C], f32r)
        VK_lo = sb("VK_lo", [P, C], f32r)
        identity = sb("identity", [P, P])
        fold_halves = sb("fold_halves", [P, P])
        group_mean = sb("group_mean", [P, P])
        all_n = sb("all_n", [P, P])
        bn = sb("bn", [P, CC, TILES, 6])
        mv = sb("mv", [P, CC, 2])
        dev = sb("dev", [P, CC])
        e2 = sb("e2", [P, CC])
        gvar = sb("gvar", [P, CC])
        minus_half = sb("minus_half", [P, CC])
        dev2 = sb("dev2", [P, CC])
        beta_mean = sb("beta_mean", [P, CC, 2])
        b_raw = sb("b_raw", [P, 1])
        gamma_col = sb("gamma_col", [P, 1])
        kmean = sb("kmean", [P, 1])
        ksum_rows = sb("ksum_rows", [P, P])
        neg_mean = [sb(f"neg_mean{i}", [P, CC]) for i in range(2)]
        scale_a = [sb(f"scale_a{i}", [P, CC]) for i in range(2)]
        scale_a1 = [sb(f"scale_a1{i}", [P, CC]) for i in range(2)]
        beta = [sb(f"beta{i}", [P, CC]) for i in range(2)]
        b_fold = [sb(f"b_fold{i}", [P, 1]) for i in range(2)]
        ksum_all = sb("ksum_all", [P, P])
        ksum_hl = sb("ksum_hl", [P, P], f32r)
        bv_hl = sb("bv_hl", [P, C], f32r)
        bv_all = xT_whole[:, :]
        bv_rows = sb("bv_rows", [P, 2])

        Wv_nat = X[1][:, 0, 0:CC * C].rearrange("p (o c) -> p o c", c=C)
        W_nat = X[1][:, 1, 0:C]

        ps_qk = [pb(f"ps_qk{i}", [P, TN]) for i in range(2)]
        ps_xT = [pb(f"ps_xT{i}", [P, C]) for i in range(2)]
        ps_kT = pb("ps_kT", [P, TN])
        ps_S = pb("ps_S", [P, C])
        ps_ring = [pb(f"ps_ring{i}", [P, TN]) for i in range(2)]

        s_weights = sem("s_weights")
        s_wv = sem("s_wv")
        s_small = sem("s_small")
        s_bv = sem("s_bv")
        s_x = [[sem(f"s_x{i}_{r}") for r in range(PARTS)] for i in range(2)]
        s_y = [sem(f"s_y{r}") for r in range(PARTS)]
        s_const0 = sem("s_const0")
        s_const = sem("s_const")
        s_wt = sem("s_wt")
        s_wc = sem("s_wc")
        s_bn = sem("s_bn")
        s_mean = sem("s_mean")
        s_scale = sem("s_scale")
        s_stat = sem("s_stat")
        s_sprod = sem("s_sprod")
        s_taken = sem("s_taken")
        s_fold = sem("s_fold")
        s_proj = sem("s_proj")
        s_xT = sem("s_xT")
        s_kT = sem("s_kT")
        s_S = sem("s_S")
        s_k = sem("s_k")
        s_qhi = sem("s_qhi")
        s_qlo = sem("s_qlo")
        s_kThi = sem("s_kThi")
        s_kTlo = sem("s_kTlo")
        s_xThi = sem("s_xThi")
        s_xTwhole = sem("s_xTwhole")
        s_xTlo = [sem("s_xTlo_dve"), sem("s_xTlo_pool")]
        s_sum = sem("s_sum")
        s_ring = sem("s_ring")
        s_free = sem("s_free")
        s_res = sem("s_res")

        s_klow = sem("s_klow")
        s_kb = sem("s_kb")

        s_passed = sem("s_passed")

        block = ctx.enter_context(nc.Block())

        def tile_no(p, t):
            return p * TILES + t

        def step_no(p, s):
            return p * STEPS + s

        def settle(eng):
            eng.sem_inc(s_passed, 1)

        def q_tile(parity, t):
            return q_own[parity][:, t, :] if t < Q_OWN else q_shared[:, t - Q_OWN, :]

        def low_no(p, s):
            return p * LOW_BY.count(LOW_BY[s]) + LOW_BY[:s].count(LOW_BY[s])

        def is_int(v):
            return isinstance(v, int)

        def ring_small(p, k):
            return (p - 1) * RING + k

        def ring_out(p, u):
            return ring_small(p, RING_SMALL + u)

        def out_banks(tail):
            return ps_ring + ps_qk if tail else ps_ring

        def ring_read(number):
            return number + 3

        SMALL_LOADS = 4
        SCALE = 4
        STAT = 2
        TAKEN = 3
        SMALL = 2

        def periods(eng, period):
            period(0, 0)
            with eng.Fori(0, IMAGES // 2 - 1) as it:
                period(it * 2 + 1, 1)
                period(it * 2 + 2, 0)
            period(IMAGES - 1, 1)
            period(IMAGES, 0)

        def wait_count(eng, s, value):
            if not is_int(value) or value > 0:
                eng.wait_ge(s, value)

        @block.sync
        def _(sp):
            sp.dma_start(W_nat[0:D, :], Wq).then_inc(s_weights, 16)
            sp.dma_start(W_nat[D:P, :], Wk).then_inc(s_weights, 16)

            def part(array, r):
                t, c = r * PART // CC, r * PART % CC
                return array[:, c:c + PART, t * TN:(t + 1) * TN]

            def load(p, buffer, r):
                sp.dma_start(part(X[buffer], r), part(x_v[p], r)).then_inc(s_x[buffer][r], 16)

            for r in range(PARTS):
                load(0, 0, r)
                if r == CC - 1:
                    with nc.allow_non_contiguous_dma(reason="one bias per partition"):
                        sp.dma_start(b_raw[0:D, :], bq.rearrange("(p a) -> p a", a=1)).then_inc(s_small, 16)
                        sp.dma_start(b_raw[D:P, :], bk.rearrange("(p a) -> p a", a=1)).then_inc(s_small, 16)
                        sp.dma_start(gamma_col[:, :], gamma.rearrange("(a n) -> a n", a=1).to_broadcast([P, 1]))\
                            .then_inc(s_small, 16)
                    sp.dma_start(bv_all, bv.rearrange("(a n) -> a n", a=1).to_broadcast([P, C])).then_inc(s_small, 16)
            sp.dma_start(Wv_nat, Wv.rearrange("(o p) c -> p o c", p=P)).then_inc(s_wv, 16)
            sp.wait_ge(s_wc, CC + 1)
            for r in range(PARTS):
                load(1, 1, r)

            def period(p, parity):
                if is_int(p) and p == 0:
                    return
                other = 1 - parity
                loads = not (is_int(p) and p >= IMAGES - 1)
                for r in range(PARTS + LOAD_LAG):
                    if r < PARTS:
                        sp.wait_ge(s_free, ring_read(ring_out(p, (r + 1) * PART - 1)))
                        sp.dma_start(part(out_v[p - 1], r), part(X[other], r)).then_inc(s_y[r], 16)
                    if loads and r >= LOAD_LAG:
                        sp.wait_ge(s_y[r - LOAD_LAG], p * 16)
                        load(p + 1, other, r - LOAD_LAG)

            periods(sp, period)
            for r in range(PARTS):
                sp.wait_ge(s_y[r], IMAGES * 16)

        @block.gpsimd
        def _(pool):
            nc.gpsimd.memset(identity[:, :], 0.0).then_inc(s_const0, 1)
            nc.gpsimd.memset(group_mean[:, :], 1.0 / GROUP).then_inc(s_const0, 1)
            nc.gpsimd.memset(minus_half[:, :], -0.5).then_inc(s_const0, 1)
            nc.gpsimd.memset(all_n[:, :], float(N)).then_inc(s_const0, 1)
            pool.wait_ge(s_const0, 4)
            nc.gpsimd.affine_select(out=identity[:, :], in_=identity[:, :], compare_op=ALU.not_equal, fill=1.0,
                                    base=0, pattern=[[-1, P]], channel_multiplier=1).then_inc(s_const, 1)
            gm = group_mean[:, :].rearrange("p (g c) -> p g c", c=GROUP)
            nc.gpsimd.affine_select(out=gm, in_=gm, compare_op=ALU.is_ge, fill=0.0, base=0,
                                    pattern=[[-GROUP, P // GROUP], [0, GROUP]], channel_multiplier=1)\
                .then_inc(s_const0, 1)
            pool.wait_ge(s_const0, 5)
            nc.gpsimd.affine_select(out=gm, in_=gm, compare_op=ALU.is_ge, fill=0.0, base=GROUP - 1,
                                    pattern=[[GROUP, P // GROUP], [0, GROUP]], channel_multiplier=-1)\
                .then_inc(s_const, 1)

            def fold(p, parity):
                a = scale_a[parity][:, :]
                pool.wait_ge(s_scale, (p + 1) * SCALE)
                nc.gpsimd.tensor_tensor(a, gvar[:, :], minus_half[:, :], ALU.pow).then_inc(s_stat, 1)
                pool.wait_ge(s_stat, p * STAT + 1)
                settle(pool)
                for c in range(CC):
                    nc.gpsimd.tensor_scalar(W_fold[parity][:, c, :], W_raw[:, c, :], scale_a[parity][:, c:c + 1],
                                            1.0, ALU.mult, ALU.mult).then_inc(s_fold, 1)
                nc.gpsimd.tensor_tensor(beta[parity][:, :], a, neg_mean[parity][:, :], ALU.mult)
                nc.gpsimd.tensor_tensor(beta_mean[:, :, 0], a, neg_mean[parity][:, :], ALU.mult)
                nc.gpsimd.tensor_tensor(beta_mean[:, :, 1], a, dev[:, :], ALU.mult)
                nc.gpsimd.tensor_scalar(scale_a1[parity][:, :], a, 1.0, 1.0, ALU.mult, ALU.add).then_inc(s_stat, 1)
                pool.wait_ge(s_stat, (p + 1) * STAT)
                settle(pool)

            def residual(p, parity, t, c):
                if c == 0:
                    pool.wait_ge(s_proj, tile_no(p, t) + 1)
                    pool.wait_ge(s_xT, step_no(p, (t + 1) * CHUNKS))
                    settle(pool)
                xs = X[parity][:, c, t * TN:(t + 1) * TN]
                nc.gpsimd.tensor_scalar(xs, xs, scale_a1[parity][:, c:c + 1], beta[parity][:, c:c + 1],
                                        ALU.mult, ALU.add).then_inc(s_res, 1)

            def ksum_times_beta(p, parity):
                pool.wait_ge(s_taken, p * TAKEN + 3)
                if not (is_int(p) and p == 0):
                    pool.wait_ge(s_free, ring_read(ring_small(p, 0)))
                settle(pool)
                for c in range(CC):
                    nc.gpsimd.tensor_scalar(ksum_beta[:, c, :], ksum_all[:, :], beta[parity][:, c:c + 1],
                                            1.0, ALU.mult, ALU.mult).then_inc(s_kb, 1)

            def xT_low(p, s):
                pool.wait_ge(s_xTwhole, low_no(p, s) + 1)
                j = s % CHUNKS
                nc.gpsimd.tensor_tensor(xT_lo[:, j, :], xT_whole[:, :], xT_hi[:, j, :].bitcast(f32),
                                        ALU.subtract).then_inc(s_xTlo[BY_POOL], 1)

            def period(p, parity):
                if is_int(p) and p == IMAGES:
                    for n in [n for at in RESIDUAL_AT for n in at if n < 0]:
                        residual(p - 1, 1 - parity, TILES + n // CC, n % CC)
                    return
                for s in range(STEPS):
                    if not (is_int(p) and p == IMAGES - 1):
                        if s == STEP_SCALE + 2:
                            fold(p + 1, 1 - parity)
                    if s == STEP_KSUM + 4:
                        ksum_times_beta(p, parity)
                    for n in RESIDUAL_AT[s]:
                        if n >= 0:
                            residual(p, parity, n // CC, n % CC)
                        elif not (is_int(p) and p == 0):
                            residual(p - 1, 1 - parity, TILES + n // CC, n % CC)
                    if LOW_BY[s] == BY_POOL:
                        xT_low(p, s)

            pool.wait_ge(s_small, SMALL_LOADS * 16)
            for k in range(2):
                row = k * D // 2
                nc.gpsimd.tensor_tensor(bv_rows[:, k:k + 1], identity[:, row:row + 1],
                                        identity[:, D + row:D + row + 1], ALU.add)
            bv_halves = [[xT_hi[:, k, :], xT_lo[:, k, :]] for k in range(2)]
            nc.gpsimd.tensor_scalar(bv_halves[0][0], bv_all, 1.0, 1.0, ALU.mult, ALU.mult).then_inc(s_bv, 1)
            pool.wait_ge(s_bv, 1)
            nc.gpsimd.tensor_tensor(bv_halves[0][1], bv_all, bv_halves[0][0].bitcast(f32), ALU.subtract)\
                .then_inc(s_bv, 1)
            pool.wait_ge(s_bv, 2)
            for k in range(2):
                nc.gpsimd.tensor_scalar(bv_halves[1][k], bv_halves[0][k].bitcast(f32), bv_rows[:, k:k + 1], 1.0,
                                        ALU.mult, ALU.mult).then_inc(s_bv, 1)
            pool.wait_ge(s_bv, 4)
            nc.gpsimd.tensor_tensor(bv_hl[:, :], bv_halves[1][0].bitcast(f32), bv_halves[1][1].bitcast(f32),
                                    ALU.add).then_inc(s_bv, 1)

            pool.wait_ge(s_wc, 1)
            fold(0, 0)
            periods(pool, period)

        @block.scalar
        def _(act):
            act.wait_ge(s_bv, 5)
            act.wait_ge(s_small, SMALL_LOADS * 16)

            def k_out(p, parity, t):
                n = tile_no(p, t)
                if t == 0:
                    act.wait_ge(s_taken, p * TAKEN + 1)
                act.wait_ge(s_proj, n + 1)
                wait_count(act, s_kT, n)
                nc.scalar.activation(k_nat, ps_qk[t % 2][D:P, :], ACT.Identity, bias=b_fold[parity][D:P, :])\
                    .then_inc(s_k, 1)

            def q_high(p, parity, t):
                if t >= Q_OWN and not (is_int(p) and p == 0):
                    act.wait_ge(s_ring, ring_out(p, (t + 1) * CC))
                nc.scalar.activation(q_tile(parity, t)[0:D, :], ps_qk[t % 2][0:D, :], ACT.Identity,
                                     bias=b_fold[parity][0:D, :]).then_inc(s_qhi, 1)

            def kT_high(p, t):
                n = tile_no(p, t)
                act.wait_ge(s_kT, n + 1)
                wait_count(act, s_S, (n - 1) * CHUNKS)
                nc.scalar.activation(kT_hl[t % 2][:, :, 0:D], ps_kT[:, 0:CHUNKS * D].rearrange("p (j d) -> p j d", d=D),
                                     ACT.Copy).then_inc(s_kThi, 1)

            def xT_high(p, s):
                g = step_no(p, s)
                act.wait_ge(s_xT, g + 1)
                wait_count(act, s_S, g - LAG + 1)
                nc.scalar.activation(xT_hi[:, s % CHUNKS, :], ps_xT[s % 2][:, :], ACT.Copy).then_inc(s_xThi, 1)

            def xT_for_pool(p, s):
                if LOW_BY[s] == BY_POOL:
                    wait_count(act, s_xTlo[BY_POOL], low_no(p, s))
                    nc.scalar.activation(xT_whole[:, :], ps_xT[s % 2][:, :], ACT.Copy).then_inc(s_xTwhole, 1)

            def statistics_taken(p, parity, k):
                act.wait_ge(s_sprod, p * STAT_PRODUCTS + k + 1)
                if k == 2:
                    nc.scalar.activation(b_fold[parity][:, :], ps_ring[0][:, 0:1], ACT.Identity, bias=b_raw[:, :])
                    nc.scalar.activation(kmean[:, :], ps_ring[0][:, 1:2], ACT.Identity, bias=b_raw[:, :])\
                        .then_inc(s_taken, 1)
                    act.wait_ge(s_taken, p * TAKEN + 1)
                    nc.scalar.activation(ksum_rows[:, :], fold_halves[:, :], ACT.Copy, scale=kmean[:, :])\
                        .then_inc(s_taken, 1)
                if k == 3:
                    wait_count(act, s_kb, p * CC)
                    wait_count(act, s_klow, p)
                    nc.scalar.activation(ksum_all[:, :], ps_kT[:, 0:P], ACT.Copy)
                    nc.scalar.activation(ksum_hl[:, :], ps_kT[:, 0:P], ACT.Copy).then_inc(s_taken, 1)

            def period(p, parity):
                tail = is_int(p) and p == IMAGES
                last = is_int(p) and p == IMAGES - 1
                for s in range(0 if tail else STEPS):
                    if s + 1 in TILE_OUT_AT:
                        k_out(p, parity, TILE_OUT_AT[s + 1])
                    if s in TILE_OUT_AT:
                        kT_high(p, TILE_OUT_AT[s])
                    xT_high(p, s)
                    if s + 1 in TILE_OUT_AT:
                        q_high(p, parity, TILE_OUT_AT[s + 1])
                    xT_for_pool(p, s)
                    if s == 0:
                        statistics_taken(p, parity, 2)
                    if s == STEP_KSUM:
                        statistics_taken(p, parity, 3)

            periods(act, period)

        @block.tensor
        def _(pe):
            pe.wait_ge(s_const, 2)
            pe.wait_ge(s_weights, 2 * 16)
            for c in range(CC):
                last = nc.tensor.transpose(ps_xT[0][:, c * P:(c + 1) * P], W_nat[:, c * P:(c + 1) * P],
                                           identity[:, :])
            last.then_inc(s_wt, 1)

            def transpose_wv(c):
                if c == 0:
                    pe.wait_ge(s_wv, 16)
                    pe.wait_ge(s_scale, SCALE)
                    pe.wait_ge(s_taken, 1)
                if c >= 2:
                    pe.wait_ge(s_wc, c)
                for o in range(CC):
                    last = nc.tensor.transpose(ps_ring[c % 2][:, o * P:(o + 1) * P],
                                               Wv_nat[:, o, c * P:(c + 1) * P], identity[:, :])
                last.then_inc(s_wt, 1)

            def project(p, parity, t, c):
                if c == 0:
                    n = tile_no(p, t)
                    wait_count(pe, s_k, n - 1)
                    wait_count(pe, s_qlo, n - 1)
                if t == 0:
                    pe.wait_ge(s_fold, p * CC + c + 1)
                mm = nc.tensor.matmul(ps_qk[t % 2][:, :], W_fold[parity][:, c, :],
                                      X[parity][:, c, t * TN:(t + 1) * TN], start=(c == 0), stop=(c == CC - 1))
                if c == CC - 1:
                    mm.then_inc(s_proj, 1)

            def transpose_x(p, parity, s):
                if s >= 2 or not (is_int(p) and p == 0):
                    before = (p, s - 2) if s >= 2 else (p - 1, STEPS + s - 2)
                    pe.wait_ge(s_xTwhole if LOW_BY[before[1]] == BY_POOL else s_xTlo[BY_DVE], low_no(*before) + 1)
                for c in range(CC):
                    last = nc.tensor.transpose(ps_xT[s % 2][:, c * P:(c + 1) * P],
                                               X[parity][:, c, s * P:(s + 1) * P], identity[:, :])
                last.then_inc(s_xT, 1)

            def transpose_k(p, t):
                n = tile_no(p, t)
                pe.wait_ge(s_k, n + 1)
                wait_count(pe, s_kTlo, n)
                if t == KSUM_TILES:
                    pe.wait_ge(s_taken, p * TAKEN + 3)
                settle(pe)
                for j in range(CHUNKS):
                    last = nc.tensor.transpose(ps_kT[:, j * D:(j + 1) * D], k_nat[:, j * P:(j + 1) * P],
                                               identity[D:P, D:P])
                last.then_inc(s_kT, 1)

            def x_kT(p, s):
                t, j = s // CHUNKS, s % CHUNKS
                if j == 0:
                    pe.wait_ge(s_kTlo, tile_no(p, t) + 1)
                if s == 0:
                    wait_count(pe, s_sum, (p - 1) * SMALL + 1)
                pe.wait_ge(s_xTlo[LOW_BY[s]], low_no(p, s) + 1)
                nc.tensor.matmul(ps_S[:, :], kT_hl[t % 2][:, j, :], xT_hi[:, j, :], start=(s == 0), stop=False)
                nc.tensor.matmul(ps_S[:, :], kT_hl[t % 2][:, j, :], xT_lo[:, j, :], start=False,
                                 stop=(s == STEPS - 1)).then_inc(s_S, 1)

            def product_j(p):
                number = ring_small(p, 0)
                pe.wait_ge(s_free, ring_read(number - 2))
                pe.wait_ge(s_sum, (p - 1) * SMALL + 1)
                for c in range(CC):
                    last = nc.tensor.matmul(ps_ring[0][:, c * P:(c + 1) * P], ST[:, c * P:(c + 1) * P],
                                            fold_halves[:, :], start=True, stop=True)
                last.then_inc(s_ring, 1)

            def product_vk(p, other):
                number = ring_small(p, 1)
                pe.wait_ge(s_free, ring_read(number - 2))
                pe.wait_ge(s_klow, p)
                nc.tensor.matmul(ps_ring[1][:, :], ksum_hl[:, :], bv_hl[:, :], start=True, stop=False)
                pe.wait_ge(s_free, ring_read(ring_small(p, 0)))
                for c in range(CC):
                    last = nc.tensor.matmul(ps_ring[1][:, :], SC[:, c, :], WvT[:, c, :], start=False,
                                            stop=(c == CC - 1))
                last.then_inc(s_ring, 1)

            def sums(p, s, first, tail):
                for step in SUM_AT[s]:
                    if step < 0 and not first:
                        x_kT(p - 1, STEPS + step)
                    if step >= 0 and not tail:
                        x_kT(p, step)

            def output_unit(p, other, u):
                t, c = u // CC, u % CC
                number = ring_out(p, u)
                if u == 0:
                    pe.wait_ge(s_qlo, p * TILES)
                    pe.wait_ge(s_sum, p * SMALL)
                banks = out_banks(is_int(p) and p == IMAGES)
                if u < 2 or u >= len(banks):
                    pe.wait_ge(s_free, ring_read(number - (2 if u < 2 else len(banks))))
                q = q_tile(other, t)
                bank = banks[u % len(banks)]
                nc.tensor.matmul(bank[:, :], VK_hi[:, c * P:(c + 1) * P], q, start=True, stop=False)
                if u == 0:
                    pe.wait_ge(s_free, ring_read(ring_small(p, 1)))
                nc.tensor.matmul(bank[:, :], VK_lo[:, c * P:(c + 1) * P], q, start=False, stop=True)\
                    .then_inc(s_ring, 1)

            def statistics_product(p, k):
                bank = ps_ring[k % 2] if k < 3 else ps_kT
                if k == 0:
                    if is_int(p) and p == 1:
                        pe.wait_ge(s_wc, CC + 1)
                    if not (is_int(p) and p <= 1):
                        pe.wait_ge(s_free, ring_read(ring_small(p, 0) - 1))
                    pe.wait_ge(s_mean, p + 1)
                    last = nc.tensor.matmul(bank[:, 0:CC], group_mean[:, :], mv[:, :, 0], start=True, stop=True)
                if k == 1:
                    pe.wait_ge(s_scale, p * SCALE + 3)
                    last = nc.tensor.matmul(bank[:, 0:CC], group_mean[:, :], e2[:, :], start=True, stop=True)
                if k == 2:
                    pe.wait_ge(s_stat, (p + 1) * STAT)
                    for c in range(CC):
                        last = nc.tensor.matmul(bank[:, 0:2], W_raw[:, c, :], beta_mean[:, c, :],
                                                start=(c == 0), stop=(c == CC - 1))
                if k == 3:
                    wait_count(pe, s_kTlo, tile_no(p, KSUM_TILES))
                    pe.wait_ge(s_taken, p * TAKEN + 2)
                    last = nc.tensor.matmul(bank[:, 0:P], all_n[D:P, :], ksum_rows[D:P, :], start=True, stop=True)
                last.then_inc(s_sprod, 1)

            def period(p, parity):
                tail = is_int(p) and p == IMAGES
                first = is_int(p) and p == 0
                last = is_int(p) and p == IMAGES - 1
                other = 1 - parity
                for s in range(STEPS):
                    if s == 0:
                        sums(p, s, first, tail)
                        if not tail:
                            transpose_x(p, parity, s)
                    if not tail:
                        for tile, chunk in PROJECT_AT[s]:
                            project(p, parity, tile, chunk)
                        if s == STEP_SCALE + 1 and not last:
                            statistics_product(p + 1, 0)
                        if s > 0:
                            transpose_x(p, parity, s)
                        if s == STEP_SCALE + 2 and not last:
                            statistics_product(p + 1, 1)
                    if s == STEP_J and not first:
                        if not tail:
                            pe.wait_ge(s_taken, p * TAKEN + 1)
                            settle(pe)
                        product_j(p)
                    if s == STEP_VK and not first:
                        product_vk(p, other)
                    if not first:
                        for u in range(UNITS_BEFORE[s], UNITS_BEFORE[s + 1])[:1]:
                            output_unit(p, other, u)
                    if not tail and s in TILE_OUT_AT:
                        transpose_k(p, TILE_OUT_AT[s])
                    if s > 0:
                        sums(p, s, first, tail)
                    if not first:
                        for u in range(UNITS_BEFORE[s], UNITS_BEFORE[s + 1])[1:]:
                            output_unit(p, other, u)
                    if not tail and s == 0:
                        statistics_product(p, 2)
                    if first and s in WV_AT:
                        transpose_wv(WV_AT[s])
                    if not tail and s == STEP_KSUM:
                        statistics_product(p, 3)

            for k in range(2):
                statistics_product(0, k)
            periods(pe, period)

        @block.vector
        def _(dve):
            dve.wait_ge(s_const, 2)
            for h in range(2):
                nc.vector.tensor_tensor(fold_halves[:, h * D:(h + 1) * D], identity[:, 0:D], identity[:, D:P],
                                        ALU.add).then_inc(s_free, 1)
            dve.wait_ge(s_wt, 1)
            nc.vector.tensor_copy(W_raw[:, :, :].rearrange("p c j -> p (c j)"), ps_xT[0][:, :]).then_inc(s_wc, 1)

            def tile_stats(p, buffer, t, c):
                if c % PART == 0:
                    dve.wait_ge(s_x[buffer][(t * CC + c) // PART], (p - buffer + 2) * 8)
                nc.vector.bn_stats(bn[:, c, t, :], X[buffer][:, c, t * TN:(t + 1) * TN]).then_inc(s_bn, 1)

            def taken(number, k):
                dve.wait_ge(s_ring, number + 1)
                return ps_ring[k % 2]

            def means(p):
                dve.wait_ge(s_bn, (p + 1) * TILES * CC)
                settle(dve)
                for c in range(CC):
                    last = nc.vector.bn_aggr(mv[:, c, :], bn[:, c, :, :].rearrange("p t k -> p (t k)"))
                last.then_inc(s_mean, 1)

            def deviations(p, parity):
                dve.wait_ge(s_sprod, p * STAT_PRODUCTS + 1)
                settle(dve)
                nc.vector.tensor_scalar(neg_mean[parity][:, :], ps_ring[0][:, 0:CC], -1.0, None, ALU.mult)
                nc.vector.tensor_tensor(dev[:, :], mv[:, :, 0], ps_ring[0][:, 0:CC], ALU.subtract)\
                    .then_inc(s_scale, 1)
                dve.wait_ge(s_scale, p * SCALE + 1)
                nc.vector.tensor_tensor(dev2[:, :], dev[:, :], dev[:, :], ALU.mult).then_inc(s_scale, 1)
                dve.wait_ge(s_scale, p * SCALE + 2)
                nc.vector.tensor_tensor(e2[:, :], dev2[:, :], mv[:, :, 1], ALU.add).then_inc(s_scale, 1)

            def group_variance(p):
                dve.wait_ge(s_sprod, p * STAT_PRODUCTS + 2)
                settle(dve)
                nc.vector.tensor_scalar(gvar[:, :], ps_ring[1][:, 0:CC], EPS, None, ALU.add)\
                    .then_inc(s_scale, 1)

            def q_low(p, parity, t):
                q = q_tile(parity, t)
                dve.wait_ge(s_qhi, tile_no(p, t) + 1)
                nc.vector.scalar_tensor_tensor(out=q[D:P, :], in0=ps_qk[t % 2][0:D, :],
                                               scalar=b_fold[parity][0:D, :],
                                               in1=q[0:D, :].bitcast(f32),
                                               op0=ALU.add, op1=ALU.subtract).then_inc(s_qlo, 1)

            def kT_low(p, t):
                dve.wait_ge(s_kThi, tile_no(p, t) + 1)
                nc.vector.tensor_tensor(kT_hl[t % 2][:, :, D:P],
                                        ps_kT[:, 0:CHUNKS * D].rearrange("p (j d) -> p j d", d=D),
                                        kT_hl[t % 2][:, :, 0:D].bitcast(f32), ALU.subtract).then_inc(s_kTlo, 1)

            def xT_low(p, s):
                j = s % CHUNKS
                dve.wait_ge(s_xThi, step_no(p, s) + 1)
                nc.vector.tensor_tensor(xT_lo[:, j, :], ps_xT[s % 2][:, :], xT_hi[:, j, :].bitcast(f32),
                                        ALU.subtract).then_inc(s_xTlo[BY_DVE], 1)

            def gather_sum(p):
                dve.wait_ge(s_S, p * STEPS)
                nc.vector.tensor_copy(ST[:, :], ps_S[:, :]).then_inc(s_sum, 1)

            def normalise_sum(p, other):
                bank = taken(ring_small(p, 0), 0)
                dve.wait_ge(s_kb, p * CC)
                for c in range(CC):
                    last = nc.vector.scalar_tensor_tensor(out=SC[:, c, :], in0=bank[:, c * P:(c + 1) * P],
                                                          scalar=scale_a[other][:, c:c + 1],
                                                          in1=ksum_beta[:, c, :], op0=ALU.mult, op1=ALU.add)
                last.then_inc(s_free, 1)

            def split_vk(p):
                dve.wait_ge(s_small, SMALL_LOADS * 16)
                bank = taken(ring_small(p, 1), 1)
                nc.vector.tensor_scalar(VK_hi[:, :], bank[:, :], gamma_col[:, :], None, ALU.mult)\
                    .then_inc(s_sum, 1)
                dve.wait_ge(s_sum, p * SMALL)
                nc.vector.scalar_tensor_tensor(out=VK_lo[:, :], in0=bank[:, :], scalar=gamma_col[:, :],
                                               in1=VK_hi[:, :].bitcast(f32), op0=ALU.mult, op1=ALU.subtract)\
                    .then_inc(s_free, 1)

            def result(p, other, u):
                t, c = u // CC, u % CC
                dve.wait_ge(s_ring, ring_out(p, u) + 1)
                banks = out_banks(is_int(p) and p == IMAGES)
                bank = banks[u % len(banks)]
                dve.wait_ge(s_res, ((p - 1) * TILES + t) * CC + c + 1)
                y = X[other][:, c, t * TN:(t + 1) * TN]
                nc.vector.tensor_tensor(y, bank[:, :], y, ALU.add).then_inc(s_free, 1)

            def period(p, parity):
                tail = is_int(p) and p == IMAGES
                first = is_int(p) and p == 0
                last = is_int(p) and p == IMAGES - 1
                other = 1 - parity
                for s in range(STEPS):
                    if s == STEP_SUM and not first:
                        gather_sum(p)
                    if not tail and not last:
                        if s == STEP_SCALE + 1:
                            deviations(p + 1, other)
                        if s == STEP_SCALE + 2:
                            group_variance(p + 1)
                    if s in TILE_OUT_AT and not tail:
                        q_low(p, parity, TILE_OUT_AT[s])
                        kT_low(p, TILE_OUT_AT[s])
                    if not first:
                        if s == STEP_J:
                            normalise_sum(p, other)
                        if s == STEP_VK:
                            split_vk(p)
                        for u in range(UNITS_BEFORE[s], UNITS_BEFORE[s + 1]):
                            result(p, other, u)
                    if not tail:
                        if LOW_BY[s] == BY_DVE:
                            xT_low(p, s)
                        if s == STEP_KSUM + 1:
                            dve.wait_ge(s_taken, p * TAKEN + 3)
                            nc.vector.tensor_tensor(ksum_hl[D:P, :], ksum_all[D:P, :], ksum_hl[D:P, :].bitcast(f32),
                                                    ALU.subtract).then_inc(s_klow, 1)
                        if not last:
                            if first and s in WV_AT:
                                c = WV_AT[s]
                                dve.wait_ge(s_wt, c + 2)
                                nc.vector.tensor_copy(WvT[:, c, :], ps_ring[c % 2][:, :]).then_inc(s_wc, 1)
                            for tile, chunk in STATS_AT[s]:
                                tile_stats(p + 1, other, tile, chunk)
                            if s == STEP_SCALE - 1:
                                means(p + 1)

            for t in range(TILES):
                for c in range(CC):
                    tile_stats(0, 0, t, c)
            means(0)
            deviations(0, 0)
            group_variance(0)
            periods(dve, period)


_INS = ['x', 'L0_conv_Wq', 'L0_conv_bq', 'L0_conv_Wk', 'L0_conv_bk', 'L0_conv_Wv', 'L0_conv_bv', 'L0_conv_gamma']


def kernel(**inputs):
    import numpy as _np
    import concourse.bacc as _bacc
    from concourse import mybir as _mybir
    from concourse.bass_utils import run_bass_kernel_spmd as _run

    nc = _bacc.Bacc("TRN2", target_bir_lowering=False, num_devices=1)
    arrays, args = {}, []
    for name in _INS:
        a = _np.ascontiguousarray(inputs[name])
        arrays[f"in_{name}_dram"] = a
        args.append(nc.dram_tensor(f"in_{name}_dram", a.shape, _mybir.dt.from_np(a.dtype), kind="ExternalInput").ap())
    shape, dtype = inputs['x'].shape, _mybir.dt.from_np(_np.dtype('float32'))
    args.append(nc.dram_tensor("out_0_dram", shape, dtype, kind="ExternalOutput").ap())
    bass_groupnorm_linear_attention(nc, *args)
    r = _run(nc, [arrays], core_ids=[0])
    return r.results[0]["out_0_dram"]
```
